# Optimizing a Trainium2 kernel written in Bass

```python
import numpy as np
import jax
import jax.numpy as jnp

def _softmax(x, axis=-1):
    return jax.nn.softmax(x, axis=axis)

def _gelu(x):
    return jax.nn.gelu(x, approximate=True)

def _silu(x):
    return jax.nn.silu(x)

def _sigmoid(x):
    return jax.nn.sigmoid(x)

def _layernorm(x, axis=-1, eps=1e-05):
    m = jnp.mean(x, axis=axis, keepdims=True)
    v = jnp.var(x, axis=axis, keepdims=True)
    return (x - m) / jnp.sqrt(v + eps)

def _scatter_add(tgt, idx, src, axis=0):
    return tgt.at[idx].add(src)

def _segment_sum(src, seg, n):
    return jax.ops.segment_sum(src, seg, n)
kernel_name = 'mk_xattn_ffn_d1_seqx_r8_9993b8'

def setup_inputs(seed: int=0):
    np.random.seed(seed)
    _w = jnp.asarray

    def _rec_inputs():
        import jax
        import jax.numpy as jnp
        _rk = jax.random.key(seed)
        x = -0.0002928 + 1 * jax.random.normal(jax.random.fold_in(_rk, 1), (8, 256, 128), jnp.float32)
        _lenS = 256 - jax.random.randint(jax.random.fold_in(_rk, 7), (8,), 0, max(1, 256 // 4) + 1, jnp.int32)
        _lenS2 = 256 - jax.random.randint(jax.random.fold_in(_rk, 8), (8,), 0, max(1, 256 // 4) + 1, jnp.int32)
        _ctx_512P = jax.random.normal(jax.random.fold_in(_rk, 11), (8, 16, 64), jnp.float32)
        _ctx_512c = jax.random.dirichlet(jax.random.fold_in(_rk, 511), 0.3 * jnp.ones((16,), jnp.float32), (8, 256))
        _ctx_512t = jnp.einsum('bsk,bkd->bsd', _ctx_512c, _ctx_512P)
        _ctx_512t = _ctx_512t * jax.lax.rsqrt(jnp.mean(jnp.square(_ctx_512t)) + 1e-12) * 0.953939
        ctx_512 = 0.00222621 + 0.99962 * (_ctx_512t + 0.3 * jax.random.normal(jax.random.fold_in(_rk, 611), (8, 256, 64), jnp.float32))
        return (x, ctx_512)
    x, ctx_512 = _rec_inputs()

    def _L0_xattn_setup():
        import jax, jax.numpy as jnp
        import numpy as np
        B, T, TC, C, CC, H = (2, 256, 64, 128, 64, 16)
        D = C // H

        def _heads(t):
            b, l, _ = t.shape
            return t.reshape(b, l, H, D).transpose(0, 2, 1, 3)
        key = jax.random.key(seed)
        ks = jax.random.split(key, 18)
        w = lambda k, i, o: jax.random.normal(k, (i, o), jnp.float32) / np.sqrt(i).astype(np.float32)
        return {'x': jax.random.normal(ks[0], (B, T, C), jnp.float32), 'cross_input': jax.random.normal(ks[1], (B, TC, CC), jnp.float32), 'Wk': w(ks[2], C, C), 'bk': jnp.zeros((C,), jnp.float32), 'Wq': w(ks[3], C, C), 'bq': jnp.zeros((C,), jnp.float32), 'Wv': w(ks[4], C, C), 'bv': jnp.zeros((C,), jnp.float32), 'Wck': w(ks[5], CC, C), 'bck': jnp.zeros((C,), jnp.float32), 'Wcq': w(ks[6], C, C), 'bcq': jnp.zeros((C,), jnp.float32), 'Wcv': w(ks[7], CC, C), 'bcv': jnp.zeros((C,), jnp.float32), 'Wp': w(ks[8], C, C), 'bp': jnp.zeros((C,), jnp.float32)}
    _L0_xattn_all = _L0_xattn_setup()
    _L0_xattn_in = {k: v for k, v in _L0_xattn_all.items() if k in ('Wk', 'bk', 'Wq', 'bq', 'Wv', 'bv', 'Wck', 'bck', 'Wcq', 'bcq', 'Wcv', 'bcv', 'Wp', 'bp')}
    del _L0_xattn_all

    def _L0_ffn_setup():
        import jax, jax.numpy as jnp
        import numpy as np
        N_EXPERTS = 8
        TOP_K = 2
        D_MODEL = 128
        HIDDEN = 512
        ROUTED_H = 128
        BATCH, SEQ = (2, 512)
        key = jax.random.key(seed)
        ks = jax.random.split(key, 8)
        std = 0.02
        return {'x': jax.random.normal(ks[0], (BATCH, SEQ, D_MODEL), dtype=jnp.float32), 'w12': std * jax.random.normal(ks[1], (N_EXPERTS, 2 * ROUTED_H, D_MODEL), dtype=jnp.float32), 'w3': std * jax.random.normal(ks[2], (N_EXPERTS, D_MODEL, ROUTED_H), dtype=jnp.float32), 'shared_w1': std * jax.random.normal(ks[3], (HIDDEN, D_MODEL), dtype=jnp.float32), 'shared_w2': std * jax.random.normal(ks[4], (HIDDEN, D_MODEL), dtype=jnp.float32), 'shared_w3': std * jax.random.normal(ks[5], (D_MODEL, HIDDEN), dtype=jnp.float32), 'router_w': std * jax.random.normal(ks[6], (N_EXPERTS, D_MODEL), dtype=jnp.float32), 'expert_bias': jnp.zeros((N_EXPERTS,), dtype=jnp.float32)}
    _L0_ffn_all = _L0_ffn_setup()
    _L0_ffn_in = {k: v for k, v in _L0_ffn_all.items() if k in ('w12', 'w3', 'shared_w1', 'shared_w2', 'shared_w3', 'router_w', 'expert_bias')}
    del _L0_ffn_all
    return {'x': x, 'ctx_512': ctx_512, 'L0_xattn_Wk': _L0_xattn_in['Wk'], 'L0_xattn_bk': _L0_xattn_in['bk'], 'L0_xattn_Wq': _L0_xattn_in['Wq'], 'L0_xattn_bq': _L0_xattn_in['bq'], 'L0_xattn_Wv': _L0_xattn_in['Wv'], 'L0_xattn_bv': _L0_xattn_in['bv'], 'L0_xattn_Wck': _L0_xattn_in['Wck'], 'L0_xattn_bck': _L0_xattn_in['bck'], 'L0_xattn_Wcq': _L0_xattn_in['Wcq'], 'L0_xattn_bcq': _L0_xattn_in['bcq'], 'L0_xattn_Wcv': _L0_xattn_in['Wcv'], 'L0_xattn_bcv': _L0_xattn_in['bcv'], 'L0_xattn_Wp': _L0_xattn_in['Wp'], 'L0_xattn_bp': _L0_xattn_in['bp'], 'L0_ffn_w12': _L0_ffn_in['w12'], 'L0_ffn_w3': _L0_ffn_in['w3'], 'L0_ffn_shared_w1': _L0_ffn_in['shared_w1'], 'L0_ffn_shared_w2': _L0_ffn_in['shared_w2'], 'L0_ffn_shared_w3': _L0_ffn_in['shared_w3'], 'L0_ffn_router_w': _L0_ffn_in['router_w'], 'L0_ffn_expert_bias': _L0_ffn_in['expert_bias']}

def reference(x, ctx_512, L0_xattn_Wk, L0_xattn_bk, L0_xattn_Wq, L0_xattn_bq, L0_xattn_Wv, L0_xattn_bv, L0_xattn_Wck, L0_xattn_bck, L0_xattn_Wcq, L0_xattn_bcq, L0_xattn_Wcv, L0_xattn_bcv, L0_xattn_Wp, L0_xattn_bp, L0_ffn_w12, L0_ffn_w3, L0_ffn_shared_w1, L0_ffn_shared_w2, L0_ffn_shared_w3, L0_ffn_router_w, L0_ffn_expert_bias):
    import jax
    import jax.numpy as jnp

    def _L0_xattn_ref(x, cross_input, Wk, bk, Wq, bq, Wv, bv, Wck, bck, Wcq, bcq, Wcv, bcv, Wp, bp):
        import jax, jax.numpy as jnp
        import numpy as np
        B, T, TC, C, CC, H = (2, 256, 64, 128, 64, 16)
        D = C // H

        def _heads(t):
            b, l, _ = t.shape
            return t.reshape(b, l, H, D).transpose(0, 2, 1, 3)
        scale = np.float32(1.0 / np.sqrt(D))
        q = _heads(x @ Wq + bq)
        k = _heads(x @ Wk + bk)
        v = _heads(x @ Wv + bv)
        att = jnp.einsum('bhqd,bhkd->bhqk', q, k) * scale
        causal = jnp.tril(jnp.ones((T, T), bool))
        att = jnp.where(causal[None, None], att, -jnp.inf)
        y = jnp.einsum('bhqk,bhkd->bhqd', jax.nn.softmax(att, axis=-1), v)
        qc = _heads(x @ Wcq + bcq)
        kc = _heads(cross_input @ Wck + bck)
        vc = _heads(cross_input @ Wcv + bcv)
        attc = jnp.einsum('bhqd,bhkd->bhqk', qc, kc) * scale
        y = y + jnp.einsum('bhqk,bhkd->bhqd', jax.nn.softmax(attc, axis=-1), vc)
        y = y.transpose(0, 2, 1, 3).reshape(x.shape[0], T, C)
        return y @ Wp + bp

    def _L0_ffn_ref(x, w12, w3, shared_w1, shared_w2, shared_w3, router_w, expert_bias):
        import jax, jax.numpy as jnp
        import numpy as np
        N_EXPERTS = 8
        TOP_K = 2
        D_MODEL = 128
        HIDDEN = 512
        ROUTED_H = 128
        BATCH, SEQ = (2, 512)
        b, s, d = x.shape
        xf = x.reshape(-1, d)
        shared = jax.nn.silu(xf @ shared_w1.T) * (xf @ shared_w2.T) @ shared_w3.T
        scores = jax.nn.sigmoid(xf @ router_w.T)
        _, top_idx = jax.lax.top_k(scores + expert_bias, TOP_K)
        mask = jax.nn.one_hot(top_idx, N_EXPERTS, dtype=xf.dtype).sum(axis=-2)
        gates = scores * mask
        h12 = jnp.einsum('td,ehd->teh', xf, w12)
        h1, h2 = jnp.split(h12, 2, axis=-1)
        h = jax.nn.silu(h1) * h2 * gates[:, :, None]
        routed = jnp.einsum('teh,edh->td', h, w3)
        return (shared + routed).reshape(b, s, d)
    x = x + _L0_xattn_ref(_layernorm(x, axis=-1), ctx_512, L0_xattn_Wk, L0_xattn_bk, L0_xattn_Wq, L0_xattn_bq, L0_xattn_Wv, L0_xattn_bv, L0_xattn_Wck, L0_xattn_bck, L0_xattn_Wcq, L0_xattn_bcq, L0_xattn_Wcv, L0_xattn_bcv, L0_xattn_Wp, L0_xattn_bp)
    x = x + _L0_ffn_ref(_layernorm(x, axis=-1), L0_ffn_w12, L0_ffn_w3, L0_ffn_shared_w1, L0_ffn_shared_w2, L0_ffn_shared_w3, L0_ffn_router_w, L0_ffn_expert_bias)
    return x

_drawn_inputs = setup_inputs


def setup_inputs(seed=0):
    import zlib

    import numpy as np

    out = dict(_drawn_inputs(seed))
    spreads = {'L0_xattn_bk': (0.0, 0.8),
     'L0_xattn_bq': (0.0, 0.454),
     'L0_xattn_bv': (0.0, 0.1),
     'L0_xattn_bck': (0.0, 0.8),
     'L0_xattn_bcq': (0.0, 0.39),
     'L0_xattn_bcv': (0.0, 0.1),
     'L0_xattn_bp': (0.0, 0.1),
     'L0_ffn_expert_bias': (0.0, 0.8)}
    factors = {'L0_ffn_w12': 8.0,
     'L0_ffn_w3': 8.0,
     'L0_ffn_shared_w1': 5.61,
     'L0_ffn_shared_w2': 5.551,
     'L0_ffn_shared_w3': 5.577,
     'L0_ffn_router_w': 8.0}
    for name, (base, spread) in spreads.items():
        noise = np.random.default_rng([zlib.crc32(name.encode()), seed]).standard_normal(out[name].shape)
        drawn = base * np.exp(spread * noise) if base else spread * noise
        out[name] = jnp.asarray(drawn.astype(out[name].dtype))
    for name, factor in factors.items():
        out[name] = (out[name] * factor).astype(out[name].dtype)
    return out
```

```python
from contextlib import ExitStack

import concourse.bass as bass
from concourse import mybir

ALU = mybir.AluOpType
ACT = mybir.ActivationFunctionType
AX_X = mybir.AxisListType.X
F32 = mybir.dt.float32
F32R = mybir.dt.float32r
BF16 = mybir.dt.bfloat16

P = 128
B, T, C = 8, 256, 128
CC = 64
H, D = 16, 8
NT = T // P
GH = 4
NG = H // GH
UNITS = 2 * NG
QUAD = P // GH
EXPERTS, HID, SHARED = 8, 128, 512
CHUNKS = SHARED // HID + EXPERTS
PAIRS = CHUNKS // 2
SHARED_PAIRS = SHARED // HID // 2
SCALE = float(D) ** -0.5
EPS = 1e-5
MASKED = -1e30
ROWS = 3 * D
ONE = ROWS

SLOTS = UNITS


def max_pass(s):
    return ((s + 2) % SLOTS, 0 if s < SLOTS - 2 else 1)


def shift_of(s):
    return ((s + 1) % SLOTS, 0 if s < SLOTS - 1 else 1)


def values_of(s):
    return ((s - 1) % SLOTS, 0 if s > 0 else -1)


def placed_in(s):
    return ((s - 3) % SLOTS, 1 if s >= 3 else 0)


def pair_of(s):
    return {5: (0, -1), 6: (1, -1), 0: (2, -2), 1: (3, -2), 2: (4, -2), 3: (5, -2)}.get(s)


EARLY = [("xT", 1), ("tokens3", -1), ("yT", -1), ("vc", 0), None, ("qkc", 1), ("v", 1), None]
LATE = [("tokens2", -1), ("qk", 1), ("out", -1), ("x2T", -1), ("cT", 1), ("route", -1), ("tokens0", 0), ("tokens1", 0)]
C_USES = [use for s in range(SLOTS)
          for use in (EARLY[s], (f"place{placed_in(s)[0]}", placed_in(s)[1]), LATE[s]) if use]


Y_USES = [use for s in range(SLOTS)
          for use in ((f"shift{shift_of(s)[0]}", shift_of(s)[1]), (f"value{values_of(s)[0]}", values_of(s)[1]))]


class Turn:

    def __init__(self, eng, t, loop):
        self.eng, self.t, self.loop, self.known = eng, t, loop, {}

    def has(self, off):
        return self.loop or 0 <= self.t + off < B

    def at(self, t):
        return not self.loop and self.t == t

    def n(self, off, part=1, of=1):
        if not self.loop:
            return of * (self.t + off) + part
        key = (of, of * off + part)
        if key not in self.known:
            self.known[key] = self.eng.snap(self.t * of + (of * off + part))
        return self.known[key]

    def user_before(self, uses, name):
        at = [u[0] for u in uses].index(name)
        for back in range(1, 2 * len(uses)):
            turns, i = divmod(at - back, len(uses))
            off = uses[i][1] + turns
            if self.has(off):
                return uses[i][0], off
        return None


def wait(eng, sem, n):
    if not isinstance(n, int) or n > 0:
        eng.wait_ge(sem, n)


def wait_apart(eng, sem, n, passed):
    wait(eng, sem, n)
    eng.sem_inc(passed, 1)


def turns(eng, one_turn):
    for t in (-1, 0, 1):
        one_turn(Turn(eng, t, False))
    with eng.Fori(2, B - 2) as t:
        one_turn(Turn(eng, t, True))
    for t in (B - 2, B - 1, B, B + 1):
        one_turn(Turn(eng, t, False))


def attention_moe_program(nc, x, ctx_in, Wk, bk, Wq, bq, Wv, bv, Wck, bck, Wcq, bcq, Wcv, bcv, Wp, bp,
                          w12, w3, shared_w1, shared_w2, shared_w3, router_w, expert_bias, out):
    with ExitStack() as stack:
        def sb(name, shape, dt=F32):
            return stack.enter_context(nc.sbuf_tensor(name, shape, dt))

        def sem(name):
            return stack.enter_context(nc.semaphore(name))

        ident = sb("ident", [P, P])
        ident_bf = sb("ident_bf", [P, P], BF16)
        causal = sb("causal", [P, P], BF16)
        sel_build = sb("sel_build", [P, 4, NG, P])
        sel = sb("sel", [P, 4, NG, P], F32R)
        one_build = sb("one_build", [P, GH])
        one_row = sb("one_row", [P, 1])
        minus_one_row = sb("minus_one_row", [P, 1])
        half_power = sb("half_power", [P, NT])
        earlier = sb("earlier", [P, EXPERTS, EXPERTS])
        wx = sb("wx", [P, 4, C])
        wx_hi = sb("wx_hi", [P, 4, C], F32R)
        wx_lo = sb("wx_lo", [P, 4, C], F32R)
        wc = sb("wc", [CC, 2, C])
        wc_hi = sb("wc_hi", [CC, 2, C], F32R)
        wc_lo = sb("wc_lo", [CC, 2, C], F32R)
        wp = sb("wp", [P, C])
        bias_col = sb("bias_col", [P, 4])
        bias_row = sb("bias_row", [P, 3, C])
        ebias = sb("ebias", [P, EXPERTS])
        router_raw = sb("router_raw", [EXPERTS, C])
        router_hi = sb("router_hi", [P, EXPERTS], F32R)
        router_lo = sb("router_lo", [P, EXPERTS], F32R)
        w12_raw = sb("w12_raw", [P, PAIRS, 2, 2, C])
        w12_hi = sb("w12_hi", [P, PAIRS, 2, 2, HID], F32R)
        w12_lo = sb("w12_lo", [P, PAIRS, 2, 2, HID], F32R)
        w3_raw = sb("w3_raw", [P, CHUNKS, HID])
        w3T = sb("w3T", [P, CHUNKS, C])

        xin = sb("xin", [P, NT, C])
        stats1 = sb("stats1", [P, NT, 6])
        mv1 = sb("mv1", [P, NT, 2])
        var1 = sb("var1", [P, NT])
        rstd1 = sb("rstd1", [P, NT])
        xn = sb("xn", [P, NT, C])
        xT = sb("xT", [P, 2, T], F32R)
        cin = sb("cin", [P, NT, C])
        cT = sb("cT", [CC, 2, T], F32R)
        nat = sb("nat", [P, 2, 4, T], F32R)
        qk = sb("qk", [P, UNITS, 2, T], F32R)
        vs = sb("vs", [P, 2, NT, H, QUAD])
        shifts = sb("shifts", [P, NT, P])
        probs = [sb(f"probs{i}", [P, GH, 2 * T]) for i in range(2)]
        yT = sb("yT", [P, UNITS, T])
        recip = sb("recip", [P, H])
        y_tok = sb("y_tok", [P, 2, NT, C])
        y_sum = sb("y_sum", [P, NT, C])
        y_sumT = sb("y_sumT", [P, T])
        xres = sb("xres", [P, NT, C])
        xresb = sb("xresb", [P, NT, C])
        x1 = sb("x1", [P, NT, C])
        stats2 = sb("stats2", [P, NT, 6])
        mv2 = sb("mv2", [P, NT, 2])
        var2 = sb("var2", [P, NT])
        rstd2 = sb("rstd2", [P, NT])
        x2n = sb("x2n", [P, NT, C])
        x2T = sb("x2T", [P, 2, T], F32R)
        route_t = sb("route_t", [P, NT, EXPERTS])
        score = sb("score", [P, NT, EXPERTS])
        biased = sb("biased", [P, NT, EXPERTS])
        above = sb("above", [P, NT, EXPERTS, EXPERTS])
        tied = sb("tied", [P, NT, EXPERTS, EXPERTS])
        rank = sb("rank", [P, NT, EXPERTS])
        gates = sb("gates", [P, NT, EXPERTS])
        th = sb("th", [P, 2 * T])
        act1 = sb("act1", [P, 2 * T])
        hid = sb("hid", [P, 2, T])
        acc = sb("acc", [P, NT, C])

        S = stack.enter_context(nc.psum_tensor("S", [P, GH, 512], F32))
        A = stack.enter_context(nc.psum_tensor("A", [P, 512], F32))
        Bk = stack.enter_context(nc.psum_tensor("Bk", [P, 512], F32))
        Cb = stack.enter_context(nc.psum_tensor("Cb", [P, 512], F32))
        Y = stack.enter_context(nc.psum_tensor("Y", [P, T], F32))

        w_attn_in = sem("w_attn_in")
        w_bias_in = sem("w_bias_in")
        w_ffn_in = sem("w_ffn_in")
        consts = sem("consts")
        w_split = sem("w_split")
        consts_dve = sem("consts_dve")
        raw_T = sem("raw_T")
        raw_hi = sem("raw_hi")
        raw_lo = sem("raw_lo")

        dve_passed = sem("dve_passed")
        pool_passed = sem("pool_passed")
        x_in = sem("x_in")
        c_in = sem("c_in")
        xres_in = sem("xres_in")
        out_sent = sem("out_sent")

        scores = [sem(f"scores{u}") for u in range(UNITS)]
        shift_T = [sem(f"shift_T{u}") for u in range(UNITS)]
        stacked = [sem(f"stacked{u}") for u in range(UNITS)]
        valued = [sem(f"valued{u}") for u in range(UNITS)]
        ffn = [sem(f"ffn{p}") for p in range(PAIRS)]
        exped = [sem(f"exped{u}") for u in range(UNITS)]
        qk_ready = [sem(f"qk_ready{u}") for u in range(UNITS)]
        yT_ready = [sem(f"yT_ready{u}") for u in range(UNITS)]
        ffn_th = [sem(f"ffn_th{p}") for p in range(PAIRS)]
        reduced = [sem(f"reduced{u}") for u in range(UNITS)]
        shifted = [sem(f"shifted{u}") for u in range(UNITS)]
        ffn_h1 = [sem(f"ffn_h1{p}") for p in range(PAIRS)]
        hid_ready = [sem(f"hid_ready{p}") for p in range(PAIRS)]
        summed = [sem(f"summed{p}") for p in range(PAIRS)]
        SUM_STEPS = [1] * SHARED_PAIRS + [2 * NT] * (PAIRS - SHARED_PAIRS)
        masked = [sem(f"masked{u}") for u in range(NG)]

        ln1 = sem("ln1")
        rstd1_ready = sem("rstd1_ready")
        xT_ps, xT_hi, xT_lo = sem("xT_ps"), sem("xT_hi"), sem("xT_lo")
        cT_ps, cT_hi, cT_lo = sem("cT_ps"), sem("cT_hi"), sem("cT_lo")
        proj_ps = [sem("proj_x_ps"), sem("proj_c_ps")]
        proj_hi = [sem("proj_x_hi"), sem("proj_c_hi")]
        proj_lo = [sem("proj_x_lo"), sem("proj_c_lo")]
        v_ps = [sem("v_ps"), sem("vc_ps")]
        v_ready = [sem("v_ready"), sem("vc_ready")]
        tokens = sem("tokens")
        recip_ready = sem("recip_ready")
        normed = sem("normed")
        y_summed = sem("y_summed")
        yT_ps, yT_sb = sem("yT_ps"), sem("yT_sb")
        xresb_ready = sem("xresb_ready")
        out_ps = sem("out_ps")
        ln2 = sem("ln2")
        rstd2_ready = sem("rstd2_ready")
        x2T_ps, x2T_hi, x2T_lo = sem("x2T_ps"), sem("x2T_hi"), sem("x2T_lo")
        route_ps, route_th = sem("route_ps"), sem("route_th")
        routed = sem("routed")

        c_free = {f"place{u}": (qk_ready[u], 1, 1) for u in range(UNITS)}
        c_free |= {f"tokens{i}": (normed, i + 1, 4) for i in range(4)}
        c_free |= {"xT": (xT_lo, 1, 1), "vc": (v_ready[1], 1, 1), "v": (v_ready[0], 1, 1),
                   "yT": (yT_sb, 1, 1), "qk": (proj_lo[0], 2, 2), "qkc": (proj_lo[1], 2, 2),
                   "out": (ln2, 1, 7), "cT": (cT_lo, 1, 1), "x2T": (x2T_lo, 1, 1),
                   "route": (route_th, 1, 1)}
        y_free = {f"shift{u}": (shifted[u], 1, 1) for u in range(UNITS)}
        y_free |= {f"value{u}": (yT_ready[u], 1, 1) for u in range(UNITS)}

        def wait_bank(eng, turn, uses, free, name):
            before = turn.user_before(uses, name)
            if before is not None:
                s, part, of = free[before[0]]
                wait(eng, s, turn.n(before[1], part, of))

        def kept(u):
            return 3 * P if u < NG else 4 * P

        RAW_BANKS = PAIRS + CHUNKS // 4
        N_CONSTS = 9

        def raw_banks(s):
            return [s] if s < SLOTS - 1 else list(range(s, RAW_BANKS))

        block = stack.enter_context(nc.Block())

        @block.sync
        def _(sp):
            def load_x(b):
                sp.dma_start(xin[:, :, :], x[b].rearrange("(t p) c -> p t c", p=P)).then_inc(x_in, 16)

            def load_c(b):
                sp.dma_start(cin[:, :, 0:CC], ctx_in[b].rearrange("(t p) c -> p t c", p=P)).then_inc(c_in, 16)

            load_x(0)
            for i, w in enumerate((Wq, Wk, Wcq, Wv)):
                sp.dma_start(wx[:, i, :], w).then_inc(w_attn_in, 16)
            load_c(0)
            for i, w in enumerate((Wck, Wcv)):
                sp.dma_start(wc[:, i, :], w).then_inc(w_attn_in, 16)
            sp.dma_start(wp[:, :], Wp).then_inc(w_ffn_in, 16)
            sp.dma_start(router_raw[:, :], router_w).then_inc(w_ffn_in, 16)
            for j, w in enumerate((shared_w1, shared_w2)):
                for c in range(2):
                    sp.dma_start(w12_raw[:, 0:SHARED_PAIRS, j, c],
                                 w.rearrange("(a c p) i -> c p a i", p=P, c=2)[c]).then_inc(w_ffn_in, 16)
            for j in range(2):
                for c in range(2):
                    sp.dma_start(w12_raw[:, SHARED_PAIRS:PAIRS, j, c],
                                 w12.rearrange("(a c) (j p) i -> j c p a i", p=P, c=2)[j, c]).then_inc(w_ffn_in, 16)
            sp.dma_start(w3_raw[:, 0:SHARED // HID, :],
                         shared_w3.rearrange("d (c h) -> d c h", h=HID)).then_inc(w_ffn_in, 16)
            sp.dma_start(w3_raw[:, SHARED // HID:CHUNKS, :], w3.rearrange("e d h -> d e h")).then_inc(w_ffn_in, 16)

            def one_turn(turn):
                t = turn.t
                if turn.loop or 0 <= t + 2 < B:
                    wait(sp, ln1, turn.n(1, 6, 6))
                    load_x(t + 2)
                if turn.has(-2):
                    wait(sp, summed[PAIRS - 1], turn.n(-2, SUM_STEPS[-1], SUM_STEPS[-1]))
                    sp.dma_start(out[t - 2].rearrange("(t p) c -> p t c", p=P), acc[:, :, :]).then_inc(out_sent, 16)
                if turn.loop or 0 <= t + 2 < B:
                    wait(sp, cT_ps, turn.n(1))
                    load_c(t + 2)
                if turn.has(0):
                    wait(sp, xresb_ready, turn.n(-1))
                    sp.dma_start(xres[:, :, :], x[t].rearrange("(t p) c -> p t c", p=P)).then_inc(xres_in, 16)

            turns(sp, one_turn)
            sp.wait_ge(out_sent, 16 * B)

        @block.tensor
        def _(pe):
            def parts(dst, pairs_, skip=False):
                for i, (a, m) in enumerate(pairs_):
                    mm = nc.tensor.matmul(dst, a, m, start=(i == 0), stop=(i == len(pairs_) - 1))
                return mm

            def three(w_hi, w_lo, m_hi, m_lo):
                return [(w_hi, m_hi), (w_hi, m_lo), (w_lo, m_hi)]

            def raw_bank(i):
                if i == 0:
                    pe.wait_ge(w_ffn_in, 16 * 12)
                    nc.tensor.transpose(Bk[:, 0:EXPERTS], router_raw[:, :], ident[0:EXPERTS, 0:EXPERTS])
                wait(pe, raw_hi, i)
                wait(pe, raw_lo, min(i, PAIRS))
                for k in range(4):
                    block_ = (w12_raw[:, i, k // 2, k % 2, :] if i < PAIRS else w3_raw[:, 4 * (i - PAIRS) + k, :])
                    mm = nc.tensor.transpose(A[:, k * P:(k + 1) * P], block_, ident[:, :])
                mm.then_inc(raw_T, 1)

            def exp_scores(u, half):
                for j in (2 * half, 2 * half + 1):
                    r = slice(QUAD * j, QUAD * j + ONE + 1)
                    nc.tensor.matmul(S[:, j, 0:T], qk[r, u, 1, 0:P], qk[r, u, 0, :], start=True, stop=True)
                    q0 = P if u < NG else 0
                    mm = nc.tensor.matmul(S[:, j, T:2 * T - q0], qk[r, u, 1, P:T], qk[r, u, 0, q0:T],
                                          start=False, stop=True, skip_group_check=True)
                return mm

            def max_scores(u, half):
                js = (2 * half, 2 * half + 1)
                for j in js:
                    r = slice(QUAD * j, QUAD * j + ROWS)
                    n = P if u < NG else T
                    nc.tensor.matmul(S[:, j, T:T + n], qk[r, u, 0, 0:P], qk[r, u, 1, 0:n], start=True, stop=True)
                    mm = nc.tensor.matmul(S[:, j, 0:T], qk[r, u, 0, P:T], qk[r, u, 1, :],
                                          start=False, stop=True, skip_group_check=True)
                if u < NG:
                    for j in js:
                        mm = nc.tensor.matmul(S[:, j, P:3 * P], ident_bf[:, :],
                                              causal[:, :].unsqueeze(1).broadcast_to([P, 2, P]),
                                              start=False, stop=True, skip_group_check=True)
                return mm

            pe.wait_ge(consts, 1)

            def exp_pass(turn, s):
                if turn.has(0):
                    for half in range(2):
                        if half == 0:
                            wait(pe, shifted[s], turn.n(0))
                        un, on = shift_of(s)
                        if turn.has(on):
                            wait(pe, reduced[un], turn.n(on, half + 1, 2))
                        else:
                            wait(pe, exped[s - 1], turn.n(0, half + 1, 2))
                        exp_scores(s, half).then_inc(scores[s], 1)

            def hidden(turn, s, w):
                pr = pair_of(s)
                if pr and turn.has(pr[1]):
                    p, o = pr
                    if w == 0:
                        if p == 0:
                            wait(pe, x2T_hi, turn.n(o))
                            wait(pe, x2T_lo, turn.n(o))
                        if turn.at(1) and p == 0:
                            pe.wait_ge(raw_hi, RAW_BANKS)
                            pe.wait_ge(raw_lo, PAIRS)
                    elif p > 0:
                        wait(pe, summed[p - 1], turn.n(o, SUM_STEPS[p - 1], SUM_STEPS[p - 1]))
                    elif turn.loop or turn.t + o > 0:
                        wait(pe, summed[PAIRS - 1], turn.n(o - 1, SUM_STEPS[-1], SUM_STEPS[-1]))
                    bank = (A, Bk)[w]
                    for c in range(2):
                        mm = parts(bank[:, c * T:(c + 1) * T],
                                   three(w12_hi[:, p, w, c, :], w12_lo[:, p, w, c, :], x2T[:, 0, :], x2T[:, 1, :]))
                    mm.then_inc(ffn[p], 1)

            def shift_rows(turn, s):
                u, o = shift_of(s)
                if turn.has(o):
                    wait(pe, reduced[u], turn.n(o, 2, 2))
                    wait_bank(pe, turn, Y_USES, y_free, f"shift{u}")
                    for qt in range(NT):
                        mm = nc.tensor.transpose(Y[:, qt * P:(qt + 1) * P], shifts[:, qt, :], ident[:, :])
                    mm.then_inc(shift_T[u], 1)

            def max_pass_(turn, s):
                u, o = max_pass(s)
                if turn.has(o):
                    wait(pe, qk_ready[u], turn.n(o))
                    if turn.at(-1) and u == 0:
                        pe.wait_ge(consts_dve, 3)
                    for half in range(2):
                        if turn.has(0):
                            wait(pe, exped[s], turn.n(0, half + 1, 2))
                        elif u > 0:
                            wait(pe, reduced[u - 1], turn.n(o, half + 1, 2))
                        max_scores(u, half).then_inc(scores[u], 1)

            def stack_unit(turn, s):
                u, o = placed_in(s)
                if turn.has(o):
                    kind, g = divmod(u, NG)
                    if g == 0:
                        wait(pe, proj_hi[kind], turn.n(o, 2, 2))
                        wait(pe, proj_lo[kind], turn.n(o, 2, 2))
                    wait_bank(pe, turn, C_USES, c_free, f"place{u}")
                    for i in range(2):
                        mm = parts(Cb[:, i * T:(i + 1) * T],
                                   [(sel[:, 2 * i + k, g, :], nat[:, kind, 2 * i + k, :]) for k in range(2)])
                    mm.then_inc(stacked[u], 1)

            def values(turn, s):
                u, o = values_of(s)
                if turn.has(o):
                    wait_bank(pe, turn, Y_USES, y_free, f"value{u}")
                    wait(pe, exped[u], turn.n(o, 2, 2))
                    if u < NG:
                        wait(pe, masked[u], turn.n(o))
                    kind, g = divmod(u, NG)
                    if g == 0:
                        wait(pe, v_ready[kind], turn.n(o))
                    for kt in range(NT):
                        for j in range(GH):
                            q0 = P * kt if kind == 0 else 0
                            mm = nc.tensor.matmul(Y[QUAD * j:QUAD * (j + 1), q0:T], vs[:, kind, kt, GH * g + j, :],
                                                  probs[u % 2][:, j, kt * T:(kt + 1) * T - q0],
                                                  start=(kt == 0), stop=(kt == NT - 1))
                    mm.then_inc(valued[u], 1)

            def w3_product(turn, s):
                pr = pair_of(s)
                if pr and turn.has(pr[1]):
                    p, o = pr
                    wait(pe, hid_ready[p], turn.n(o))
                    if p < SHARED_PAIRS:
                        for tt in range(NT):
                            mm = parts(Bk[:, tt * P:(tt + 1) * P],
                                       [(hid[:, c, tt * P:(tt + 1) * P], w3T[:, 2 * p + c, :]) for c in range(2)])
                    else:
                        for c in range(2):
                            for tt in range(NT):
                                k = c * NT + tt
                                mm = parts(Bk[:, k * P:(k + 1) * P],
                                           [(hid[:, c, tt * P:(tt + 1) * P], w3T[:, 2 * p + c, :])])
                    mm.then_inc(ffn[p], 1)

            def bank_c(turn, s, use):
                if use is None or not turn.has(use[1]):
                    return
                name, o = use
                if name == "xT":
                    wait(pe, ln1, turn.n(o, 6, 6))
                    wait_bank(pe, turn, C_USES, c_free, name)
                    for tt in range(NT):
                        mm = nc.tensor.transpose(Cb[:, tt * P:(tt + 1) * P], xn[:, tt, :], ident[:, :])
                    mm.then_inc(xT_ps, 1)
                elif name == "cT":
                    wait(pe, c_in, turn.n(o, 1, 1) * 16 if not turn.loop else turn.n(o, 16, 16))
                    wait_bank(pe, turn, C_USES, c_free, name)
                    for tt in range(NT):
                        mm = nc.tensor.transpose(Cb[:, tt * P:(tt + 1) * P], cin[:, tt, :], ident[:, :])
                    mm.then_inc(cT_ps, 1)
                elif name == "x2T":
                    wait(pe, ln2, turn.n(o, 7, 7))
                    wait_bank(pe, turn, C_USES, c_free, name)
                    for tt in range(NT):
                        mm = nc.tensor.transpose(Cb[:, tt * P:(tt + 1) * P], x2n[:, tt, :], ident[:, :])
                    mm.then_inc(x2T_ps, 1)
                elif name == "yT":
                    wait(pe, y_summed, turn.n(o))
                    wait_bank(pe, turn, C_USES, c_free, name)
                    for tt in range(NT):
                        mm = nc.tensor.transpose(Cb[:, tt * P:(tt + 1) * P], y_sum[:, tt, :], ident[:, :])
                    mm.then_inc(yT_ps, 1)
                elif name in ("qk", "qkc"):
                    kind = 0 if name == "qk" else 1
                    wait(pe, w_split, 4)
                    if kind == 0:
                        wait(pe, xT_hi, turn.n(o))
                        wait(pe, xT_lo, turn.n(o))
                    else:
                        wait(pe, cT_hi, turn.n(o))
                        wait(pe, cT_lo, turn.n(o))
                    wait_bank(pe, turn, C_USES, c_free, name)
                    q = 2 * kind
                    mm = parts(Cb[:, 0:T], three(wx_hi[:, q, :], wx_lo[:, q, :], xT[:, 0, :], xT[:, 1, :]))
                    if kind == 0:
                        mm = parts(Cb[:, T:2 * T], three(wx_hi[:, 1, :], wx_lo[:, 1, :], xT[:, 0, :], xT[:, 1, :]))
                    else:
                        mm = parts(Cb[:, T:2 * T], three(wc_hi[:, 0, :], wc_lo[:, 0, :], cT[:, 0, :], cT[:, 1, :]))
                    mm.then_inc(proj_ps[kind], 1)
                elif name in ("v", "vc"):
                    kind = 0 if name == "v" else 1
                    wait_bank(pe, turn, C_USES, c_free, name)
                    src, wh, wl = ((xT, wx_hi[:, 3, :], wx_lo[:, 3, :]) if kind == 0 else
                                   (cT, wc_hi[:, 1, :], wc_lo[:, 1, :]))
                    for kt in range(NT):
                        hi, lo = (src[:, i, kt * P:(kt + 1) * P] for i in range(2))
                        mm = parts(Cb[:, kt * P:(kt + 1) * P], [(hi, wh), (lo, wh), (hi, wl)])
                    mm.then_inc(v_ps[kind], 1)
                elif name.startswith("tokens"):
                    kind, tt = divmod(int(name[-1]), NT)
                    wait(pe, yT_ready[NG * kind + NG - 1], turn.n(o))
                    wait_bank(pe, turn, C_USES, c_free, name)
                    for g in range(NG):
                        mm = nc.tensor.transpose(Cb[:, g * P:(g + 1) * P],
                                                 yT[:, NG * kind + g, tt * P:(tt + 1) * P], ident[:, :])
                    mm.then_inc(tokens, 1)
                elif name == "out":
                    wait(pe, yT_sb, turn.n(o))
                    wait_bank(pe, turn, C_USES, c_free, name)
                    for tt in range(NT):
                        mm = parts(Cb[:, tt * P:(tt + 1) * P], [(y_sumT[:, tt * P:(tt + 1) * P], wp[:, :])])
                    mm.then_inc(out_ps, 1)
                elif name == "route":
                    wait(pe, x2T_hi, turn.n(o))
                    wait(pe, x2T_lo, turn.n(o))
                    wait_bank(pe, turn, C_USES, c_free, name)
                    for tt in range(NT):
                        hi, lo = (x2T[:, i, tt * P:(tt + 1) * P] for i in range(2))
                        mm = parts(Cb[:, tt * EXPERTS:(tt + 1) * EXPERTS],
                                   [(hi, router_hi[:, :]), (lo, router_hi[:, :]), (hi, router_lo[:, :])])
                    mm.then_inc(route_ps, 1)

            def one_turn(turn):
                for s in range(SLOTS):
                    exp_pass(turn, s)
                    if pair_of(s):
                        hidden(turn, s, 0)
                        bank_c(turn, s, EARLY[s])
                        hidden(turn, s, 1)
                        shift_rows(turn, s)
                        max_pass_(turn, s)
                        stack_unit(turn, s)
                        values(turn, s)
                        w3_product(turn, s)
                    else:
                        shift_rows(turn, s)
                        stack_unit(turn, s)
                        max_pass_(turn, s)
                        values(turn, s)
                    if turn.at(0):
                        for i in raw_banks(s):
                            raw_bank(i)
                    bank_c(turn, s, LATE[s])

            turns(pe, one_turn)

        @block.scalar
        def _(act):
            for i, b_ in enumerate((bq, bk, bcq, bck)):
                act.dma_start(bias_col[:, i:i + 1], b_.rearrange("(c a) -> c a", a=1)).then_inc(w_bias_in, 16)
            for i, b_ in enumerate((bv, bcv, bp)):
                act.dma_start(bias_row[:, i, :], b_.rearrange("(a c) -> a c", a=1).broadcast_to([P, C])).then_inc(w_bias_in, 16)
            act.dma_start(ebias[:, :], expert_bias.rearrange("(a c) -> a c", a=1).broadcast_to([P, EXPERTS])).then_inc(w_bias_in, 16)
            act.wait_ge(w_bias_in, 16 * 8)

            def from_bank_c(turn, use):
                if use is None or not turn.has(use[1]):
                    return
                name, o = use
                if name == "cT":
                    wait(act, cT_ps, turn.n(o))
                    nc.scalar.copy(cT[:, 0, :], Cb[0:CC, 0:T]).then_inc(cT_hi, 1)
                elif name == "x2T":
                    wait(act, x2T_ps, turn.n(o))
                    nc.scalar.copy(x2T[:, 0, :], Cb[:, 0:T]).then_inc(x2T_hi, 1)
                elif name == "qk":
                    wait(act, proj_ps[0], turn.n(o))
                    for i in range(2):
                        nc.scalar.activation(nat[:, 0, 2 * i, :], Cb[:, i * T:(i + 1) * T], ACT.Identity,
                                             bias=bias_col[:, i:i + 1]).then_inc(proj_hi[0], 1)
                elif name == "route":
                    wait(act, route_ps, turn.n(o))
                    nc.scalar.activation(route_t[:, :, :].rearrange("p t e -> p (t e)"), Cb[:, 0:NT * EXPERTS],
                                         ACT.Tanh, scale=0.5).then_inc(route_th, 1)

            def values(turn, s):
                u, o = values_of(s)
                if turn.has(o):
                    wait(act, valued[u], turn.n(o))
                    nc.scalar.copy(yT[:, u, :], Y[:, :]).then_inc(yT_ready[u], 1)

            def one_turn(turn):
                for s in range(SLOTS):
                    if turn.has(0):
                        for half in range(2):
                            hs = slice(2 * half, 2 * half + 2)
                            wait(act, scores[s], turn.n(0, 3 + half, 4))
                            if half == 0:
                                v, o = values_of(s - 1) if s > 0 else (SLOTS - 2, -1)
                                wait(act, valued[v], turn.n(o if s != 1 else -1))
                            nc.scalar.activation(probs[s % 2][:, hs, 0:kept(s)], S[:, hs, 0:kept(s)], ACT.Exp,
                                                 scale=SCALE).then_inc(exped[s], 1)
                    pr = pair_of(s)
                    if pr and turn.has(pr[1]):
                        p, o = pr
                        wait(act, ffn[p], turn.n(o, 1, 3))
                        nc.scalar.activation(th[:, :], A[:, :], ACT.Tanh, scale=0.5).then_inc(ffn_th[p], 1)
                    u, o = placed_in(s)
                    if turn.has(o):
                        wait(act, stacked[u], turn.n(o))
                        if turn.at(-1) and u == 0:
                            act.wait_ge(consts_dve, 1)
                        nc.scalar.activation(qk[:, u, :, :], Cb[:, :].rearrange("p (i t) -> p i t", i=2), ACT.Identity,
                                             bias=one_row[:, 0:1]).then_inc(qk_ready[u], 1)
                    values(turn, s)
                    if turn.at(0):
                        for i in raw_banks(s):
                            act.wait_ge(raw_T, i + 1)
                            if i == 0:
                                nc.scalar.copy(router_hi[:, :], Bk[:, 0:EXPERTS]).then_inc(consts_dve, 1)
                            if i < PAIRS:
                                nc.scalar.copy(w12_hi[:, i].rearrange("p a b i -> p (a b i)"), A[:, :]).then_inc(raw_hi, 1)
                            else:
                                k = 4 * (i - PAIRS)
                                nc.scalar.mul(w3T[:, k:k + 4, :].rearrange("p k i -> p (k i)"), A[:, :], 0.5).then_inc(raw_hi, 1)
                    from_bank_c(turn, LATE[s])

            turns(act, one_turn)

        @block.vector
        def _(dve):
            dve.wait_ge(consts, 4)
            nc.vector.reduce_sum(one_row[:, :], one_build[:, :], AX_X).then_inc(consts_dve, 1)
            dve.wait_ge(consts_dve, 1)
            nc.vector.tensor_scalar(minus_one_row[:, :], one_row[:, :], -1.0, None, ALU.mult).then_inc(consts_dve, 1)
            nc.vector.tensor_copy(ident_bf[:, :], ident[:, :]).then_inc(consts_dve, 1)
            dve.wait_ge(consts, N_CONSTS)
            nc.vector.tensor_copy(sel[:, :, :, :].rearrange("p a g m -> p (a g m)"),
                                  sel_build[:, :, :, :].rearrange("p a g m -> p (a g m)")).then_inc(w_split, 1)
            dve.wait_ge(w_attn_in, 16 * 6)
            nc.vector.tensor_copy(wx_hi[:, :, :].rearrange("p a c -> p (a c)"),
                                  wx[:, :, :].rearrange("p a c -> p (a c)")).then_inc(w_split, 1)
            nc.vector.tensor_copy(wc_hi[:, :, :].rearrange("p a c -> p (a c)"),
                                  wc[:, :, :].rearrange("p a c -> p (a c)")).then_inc(w_split, 1)
            dve.wait_ge(w_split, 3)
            nc.vector.tensor_tensor(wx_lo[:, :, :], wx[:, :, :], wx_hi[:, :, :].bitcast(F32), ALU.subtract)
            nc.vector.tensor_tensor(wc_lo[:, :, :], wc[:, :, :], wc_hi[:, :, :].bitcast(F32), ALU.subtract).then_inc(w_split, 1)
            dve.wait_ge(w_bias_in, 16 * 8)

            def low_part(dst, src, hi):
                return nc.vector.tensor_tensor(dst, src, hi.bitcast(F32), ALU.subtract)

            def normalise(turn, off, done, base, of, src, stats, mv, dst, rstd_ready, rstd, first):
                if first:
                    for tt in range(NT):
                        nc.vector.bn_stats(stats[:, tt, :], src[:, tt, :]).then_inc(done, 1)
                    for tt in range(NT):
                        wait_apart(dve, done, turn.n(off, base + tt + 1, of), dve_passed)
                        nc.vector.bn_aggr(mv[:, tt, :], stats[:, tt, :]).then_inc(done, 1)
                else:
                    wait(dve, rstd_ready, turn.n(off, 2, 2))
                    for tt in range(NT):
                        nc.vector.tensor_scalar(dst[:, tt, :], src[:, tt, :], mv[:, tt, 0:1], rstd[:, tt:tt + 1],
                                                ALU.subtract, ALU.mult).then_inc(done, 1)

            def from_bank_c(turn, use):
                if use is None or not turn.has(use[1]):
                    return
                name, o = use
                if name == "xT":
                    wait(dve, xT_ps, turn.n(o))
                    nc.vector.tensor_copy(xT[:, 0, :], Cb[:, 0:T]).then_inc(xT_hi, 1)
                    wait(dve, xT_hi, turn.n(o))
                    low_part(xT[:, 1, :], Cb[:, 0:T], xT[:, 0, :]).then_inc(xT_lo, 1)
                elif name == "cT":
                    wait(dve, cT_hi, turn.n(o))
                    low_part(cT[:, 1, :], Cb[0:CC, 0:T], cT[:, 0, :]).then_inc(cT_lo, 1)
                elif name == "x2T":
                    wait(dve, x2T_hi, turn.n(o))
                    low_part(x2T[:, 1, :], Cb[:, 0:T], x2T[:, 0, :]).then_inc(x2T_lo, 1)
                elif name in ("qk", "qkc"):
                    kind = 0 if name == "qk" else 1
                    if kind == 1:
                        wait(dve, proj_ps[1], turn.n(o))
                        for i in range(2):
                            nc.vector.tensor_scalar(nat[:, 1, 2 * i, :], Cb[:, i * T:(i + 1) * T],
                                                    bias_col[:, 2 + i:3 + i], None, ALU.add).then_inc(proj_hi[1], 1)
                    for i in range(2):
                        wait(dve, proj_hi[kind], turn.n(o, 2, 2))
                        nc.vector.scalar_tensor_tensor(
                            out=nat[:, kind, 2 * i + 1, :], in0=Cb[:, i * T:(i + 1) * T],
                            scalar=bias_col[:, 2 * kind + i:2 * kind + i + 1], in1=nat[:, kind, 2 * i, :].bitcast(F32),
                            op0=ALU.add, op1=ALU.subtract).then_inc(proj_lo[kind], 1)
                elif name == "yT":
                    wait(dve, yT_ps, turn.n(o))
                    nc.vector.tensor_copy(y_sumT[:, :], Cb[:, 0:T]).then_inc(yT_sb, 1)
                elif name in ("v", "vc"):
                    kind = 0 if name == "v" else 1
                    wait(dve, v_ps[kind], turn.n(o))
                    if not turn.loop and turn.t + o == 0:
                        dve.wait_ge(consts, N_CONSTS)
                    for kt in range(NT):
                        r_ = nc.vector.tensor_tensor(
                            vs[:, kind, kt, :, 0:D], Cb[:, kt * P:(kt + 1) * P].rearrange("p (h d) -> p h d", d=D),
                            bias_row[:, kind, :].rearrange("p (h d) -> p h d", d=D), ALU.add)
                    r_.then_inc(v_ready[kind], 1)
                elif name.startswith("tokens"):
                    i = int(name[-1])
                    kind, tt = divmod(i, NT)
                    wait(dve, tokens, turn.n(o, i + 1, 4))
                    heads = Cb[:, :].rearrange("p (h r) -> p h r", r=QUAD)
                    nc.vector.reciprocal(recip[:, :], heads[:, :, D]).then_inc(recip_ready, 1)
                    wait(dve, recip_ready, turn.n(o, i + 1, 4))
                    nc.vector.tensor_tensor(y_tok[:, kind, tt, :].rearrange("p (h d) -> p h d", d=D),
                                            heads[:, :, 0:D],
                                            recip[:, :].unsqueeze(2).broadcast_to([P, H, D]),
                                            ALU.mult).then_inc(normed, 1)
                elif name == "out":
                    wait(dve, out_ps, turn.n(o))
                    wait(dve, xresb_ready, turn.n(o))
                    nc.vector.tensor_tensor(x1[:, :, :].rearrange("p t c -> p (t c)"), Cb[:, 0:T],
                                            xresb[:, :, :].rearrange("p t c -> p (t c)"), ALU.add).then_inc(ln2, 1)
                    wait(dve, ln2, turn.n(o, 1, 7))
                    normalise(turn, o, ln2, 1, 7, x1, stats2, mv2, x2n, rstd2_ready, rstd2, True)
                elif name == "route":
                    wait(dve, route_th, turn.n(o))
                    nc.vector.tensor_scalar(score[:, :, :], route_t[:, :, :], 0.5, 0.5, ALU.mult,
                                            ALU.add).then_inc(routed, 1)
                    wait(dve, routed, turn.n(o, 1, 8))
                    nc.vector.tensor_tensor(biased[:, :, :], score[:, :, :],
                                            ebias[:, :].unsqueeze(1).broadcast_to([P, NT, EXPERTS]),
                                            ALU.add).then_inc(routed, 1)
                    wait(dve, routed, turn.n(o, 2, 8))
                    for tt in range(NT):
                        mine = biased[:, tt, :].unsqueeze(2).broadcast_to([P, EXPERTS, EXPERTS])
                        other = biased[:, tt, :].unsqueeze(1).broadcast_to([P, EXPERTS, EXPERTS])
                        nc.vector.tensor_tensor(above[:, tt], other, mine, ALU.is_gt)
                        r_ = nc.vector.tensor_tensor(tied[:, tt], other, mine, ALU.is_equal)
                    r_.then_inc(routed, 1)
                    wait(dve, routed, turn.n(o, 3, 8))
                    nc.vector.tensor_tensor(tied[:, :, :, :], tied[:, :, :, :],
                                            earlier[:, :, :].unsqueeze(1).broadcast_to([P, NT, EXPERTS, EXPERTS]),
                                            ALU.mult).then_inc(routed, 1)
                    wait(dve, routed, turn.n(o, 4, 8))
                    nc.vector.tensor_tensor(above[:, :, :, :], above[:, :, :, :], tied[:, :, :, :],
                                            ALU.add).then_inc(routed, 1)
                    wait(dve, routed, turn.n(o, 5, 8))
                    nc.vector.reduce_sum(rank[:, :, :], above[:, :, :, :], AX_X).then_inc(routed, 1)
                    wait(dve, routed, turn.n(o, 6, 8))
                    nc.vector.tensor_scalar(rank[:, :, :], rank[:, :, :], 2.0, None, ALU.is_lt).then_inc(routed, 1)
                    wait(dve, routed, turn.n(o, 7, 8))
                    nc.vector.tensor_tensor(gates[:, :, :], rank[:, :, :], score[:, :, :],
                                            ALU.mult).then_inc(routed, 1)

            first = Turn(dve, 0, False)
            dve.wait_ge(x_in, 16)
            normalise(first, 0, ln1, 0, 6, xin, stats1, mv1, xn, rstd1_ready, rstd1, True)
            normalise(first, 0, ln1, 0, 6, xin, stats1, mv1, xn, rstd1_ready, rstd1, False)

            def one_turn(turn):
                for s in range(SLOTS):
                    from_bank_c(turn, EARLY[s])
                    pr = pair_of(s)
                    if pr and turn.has(pr[1]):
                        p, o = pr
                        wait(dve, ffn_th[p], turn.n(o))
                        nc.vector.scalar_tensor_tensor(out=act1[:, :], in0=th[:, :], scalar=1.0, in1=A[:, :],
                                                       op0=ALU.add, op1=ALU.mult).then_inc(ffn_h1[p], 1)
                        wait(dve, ffn_h1[p], turn.n(o))
                        wait(dve, ffn[p], turn.n(o, 2, 3))
                        nc.vector.tensor_tensor(hid[:, :, :].rearrange("p c t -> p (c t)"), act1[:, :], Bk[:, :],
                                                ALU.mult).then_inc(hid_ready[p], 1)
                    u, o = shift_of(s)
                    if turn.has(o):
                        wait(dve, shift_T[u], turn.n(o))
                        nc.vector.scalar_tensor_tensor(out=qk[:, u, 0, :], in0=Y[:, :], scalar=minus_one_row[:, 0:1],
                                                       in1=qk[:, u, 0, :].bitcast(F32), op0=ALU.add,
                                                       op1=ALU.add).then_inc(shifted[u], 1)
                    if s == 6 and turn.has(2):
                        wait(dve, x_in, turn.n(2, 16, 16))
                        normalise(turn, 2, ln1, 0, 6, xin, stats1, mv1, xn, rstd1_ready, rstd1, True)
                    if s == 7 and turn.has(2):
                        wait(dve, xT_ps, turn.n(1))
                        normalise(turn, 2, ln1, 0, 6, xin, stats1, mv1, xn, rstd1_ready, rstd1, False)
                    if s == 3 and turn.has(-1):
                        normalise(turn, -1, ln2, 1, 7, x1, stats2, mv2, x2n, rstd2_ready, rstd2, False)
                    u, o = max_pass(s)
                    if turn.has(o):
                        for half in range(2):
                            hs = slice(2 * half, 2 * half + 2)
                            wait(dve, scores[u], turn.n(o, half + 1, 4))
                            dst = shifts[:, :, :].rearrange("p q (j r) -> p q j r", r=QUAD)[:, :, hs, ONE]
                            if u < NG:
                                nc.vector.tensor_reduce(dst[:, 1, :], S[:, hs, 0:T], AX_X, ALU.max, negate=True)
                                nc.vector.tensor_reduce(dst[:, 0, :], S[:, hs, T:T + P], AX_X, ALU.max,
                                                        negate=True).then_inc(reduced[u], 1)
                            else:
                                for q in range(NT):
                                    r_ = nc.vector.tensor_reduce(dst[:, 1 - q, :], S[:, hs, q * T:(q + 1) * T], AX_X,
                                                                 ALU.max, negate=True)
                                r_.then_inc(reduced[u], 1)
                    if pr and turn.has(pr[1]):
                        p, o = pr
                        wait(dve, ffn[p], turn.n(o, 3, 3))
                        if p < SHARED_PAIRS:
                            if p == 0:
                                wait(dve, out_sent, turn.n(o - 1, 16, 16))
                            else:
                                wait(dve, summed[p - 1], turn.n(o))
                            before = x1 if p == 0 else acc
                            nc.vector.tensor_tensor(acc[:, :, :].rearrange("p t c -> p (t c)"), Bk[:, 0:T],
                                                    before[:, :, :].rearrange("p t c -> p (t c)"),
                                                    ALU.add).then_inc(summed[p], 1)
                        else:
                            if p == SHARED_PAIRS:
                                wait(dve, routed, turn.n(o, 8, 8))
                                wait(dve, summed[p - 1], turn.n(o))
                            else:
                                wait(dve, summed[p - 1], turn.n(o, 4, 4))
                            for c in range(2):
                                for tt in range(NT):
                                    k = c * NT + tt
                                    e = 2 * (p - SHARED_PAIRS) + c
                                    if c == 1:
                                        wait(dve, summed[p], turn.n(o, tt + 1, 4))
                                    nc.vector.scalar_tensor_tensor(out=acc[:, tt, :], in0=Bk[:, k * P:(k + 1) * P],
                                                                   scalar=gates[:, tt, e:e + 1], in1=acc[:, tt, :],
                                                                   op0=ALU.mult, op1=ALU.add).then_inc(summed[p], 1)
                    if turn.at(0):
                        for i in [i for i in raw_banks(s) if i < PAIRS]:
                            dve.wait_ge(raw_hi, i + 1)
                            if i == 0:
                                low_part(router_lo[:, :], Bk[:, 0:EXPERTS], router_hi[:, :])
                            low_part(w12_lo[:, i].rearrange("p a b i -> p (a b i)"), A[:, :],
                                     w12_hi[:, i].rearrange("p a b i -> p (a b i)")).then_inc(raw_lo, 1)
                    from_bank_c(turn, LATE[s])

            turns(dve, one_turn)

        @block.gpsimd
        def _(pool):
            def select(dst, compare, fill, base, pattern, step):
                return nc.gpsimd.affine_select(out=dst, in_=dst, compare_op=compare, fill=fill, base=base,
                                               pattern=pattern, channel_multiplier=step)

            built = sem("built")
            nc.gpsimd.memset(ident[:, :], 0.0).then_inc(built, 1)
            nc.gpsimd.memset(one_build[:, :], 0.0).then_inc(built, 1)
            nc.gpsimd.memset(causal[:, :], 0.0).then_inc(built, 1)
            nc.gpsimd.memset(cin[:, :, CC:C], 0.0).then_inc(built, 1)
            nc.gpsimd.memset(shifts[:, :, :], 0.0).then_inc(built, 1)
            nc.gpsimd.memset(sel_build[:, :, :, :], 0.0).then_inc(built, 1)
            nc.gpsimd.memset(vs[:, :, :, :, :], 0.0).then_inc(built, 1)
            nc.gpsimd.memset(earlier[:, :, :], 1.0).then_inc(built, 1)
            pool.wait_ge(built, 1)
            select(ident[:, :], ALU.not_equal, 1.0, 0, [[-1, P]], 1).then_inc(consts, 1)
            pool.wait_ge(built, 5)
            select(one_build[:, :], ALU.not_equal, 1.0, -ONE, [[-QUAD, GH]], 1).then_inc(consts, 1)
            select(causal[:, :], ALU.is_ge, MASKED, 0, [[-1, P]], 1).then_inc(consts, 1)
            nc.gpsimd.memset(half_power[:, :], -0.5).then_inc(consts, 1)
            pool.wait_ge(built, 8)
            nc.gpsimd.memset(vs[:, :, :, :, D:D + 1], 1.0).then_inc(consts, 1)
            select(earlier[:, :, :], ALU.is_gt, 0.0, 0, [[1, EXPERTS], [-1, EXPERTS]], 0).then_inc(consts, 1)
            for part, rows in ((0, (0, 1)), (1, (2,)), (2, (0, 2)), (3, (1,))):
                view = sel_build[:, part, :, :].rearrange("p g (j r) -> p g j r", r=QUAD)
                for g in range(NG):
                    for r in rows:
                        last = select(view[:, g, :, r * D:(r + 1) * D], ALU.not_equal, 1.0, -g * GH * D,
                                      [[-D, GH], [-1, D]], 1)
                if part in (0, 1, 3):
                    last.then_inc(consts, 1)
            pool.wait_ge(w_bias_in, 16 * 8)

            def rstd(turn, off, stats_done, part, of, mv, var, dst, ready):
                wait_apart(pool, stats_done, turn.n(off, part, of), pool_passed)
                nc.gpsimd.tensor_scalar(var[:, :], mv[:, :, 1], EPS, None, ALU.add).then_inc(ready, 1)
                wait(pool, ready, turn.n(off, 1, 2))
                nc.gpsimd.tensor_tensor(dst[:, :], var[:, :], half_power[:, :], ALU.pow).then_inc(ready, 1)

            rstd(Turn(pool, 0, False), 0, ln1, 4, 6, mv1, var1, rstd1, rstd1_ready)

            def one_turn(turn):
                for s in range(SLOTS):
                    if s == 3 and turn.has(-1):
                        rstd(turn, -1, ln2, 5, 7, mv2, var2, rstd2, rstd2_ready)
                    if s < NG and turn.has(0):
                        wait_apart(pool, exped[s], turn.n(0, 2, 2), pool_passed)
                        diag = probs[s % 2][:, :, :].rearrange("p h (b q) -> p h b q", b=2)[:, :, :, 0:P]
                        select(diag, ALU.is_ge, 0.0, 0, [[0, GH], [0, 2], [1, P]], -1).then_inc(masked[s], 1)
                    if s == 1 and turn.has(-1):
                        wait(pool, normed, turn.n(-1, 4, 4))
                        nc.gpsimd.tensor_tensor(y_sum[:, :, :], y_tok[:, 0], y_tok[:, 1], ALU.add).then_inc(y_summed, 1)
                        wait(pool, xres_in, turn.n(-1, 16, 16))
                        for tt in range(NT):
                            r_ = nc.gpsimd.tensor_tensor(xresb[:, tt, :], xres[:, tt, :], bias_row[:, 2, :], ALU.add)
                        r_.then_inc(xresb_ready, 1)
                    if s == 6 and turn.has(2):
                        rstd(turn, 2, ln1, 4, 6, mv1, var1, rstd1, rstd1_ready)

            turns(pool, one_turn)


_INS = ['x', 'ctx_512', 'L0_xattn_Wk', 'L0_xattn_bk', 'L0_xattn_Wq', 'L0_xattn_bq', 'L0_xattn_Wv', 'L0_xattn_bv',
        'L0_xattn_Wck', 'L0_xattn_bck', 'L0_xattn_Wcq', 'L0_xattn_bcq', 'L0_xattn_Wcv', 'L0_xattn_bcv', 'L0_xattn_Wp',
        'L0_xattn_bp', 'L0_ffn_w12', 'L0_ffn_w3', 'L0_ffn_shared_w1', 'L0_ffn_shared_w2', 'L0_ffn_shared_w3',
        'L0_ffn_router_w', 'L0_ffn_expert_bias']
_OUT = (B, T, C)


def kernel(**inputs):
    import numpy as _np
    import concourse.bacc as _bacc
    from concourse import mybir as _mybir
    from concourse.bass_utils import run_bass_kernel_spmd as _run

    nc = _bacc.Bacc("TRN2", target_bir_lowering=False, num_devices=1)
    arrays, args = {}, []
    for name in _INS:
        a = _np.ascontiguousarray(inputs[name])
        arrays[f"in_{name}_dram"] = a
        args.append(nc.dram_tensor(f"in_{name}_dram", a.shape, _mybir.dt.from_np(a.dtype), kind="ExternalInput").ap())
    args.append(nc.dram_tensor("out_0_dram", _OUT, _mybir.dt.float32, kind="ExternalOutput").ap())
    attention_moe_program(nc, *args)
    r = _run(nc, [arrays], core_ids=[0])
    return r.results[0]["out_0_dram"]
```

```python
from contextlib import ExitStack

import concourse.bass as bass
from concourse import mybir

ALU = mybir.AluOpType
ACT = mybir.ActivationFunctionType
AX_X = mybir.AxisListType.X
F32 = mybir.dt.float32
F32R = mybir.dt.float32r
BF16 = mybir.dt.bfloat16

P = 128
B, T, C = 8, 256, 128
CC = 64
H, D = 16, 8
NT = T // P
GH = 4
NG = H // GH
UNITS = 2 * NG
QUAD = P // GH
EXPERTS, HID, SHARED = 8, 128, 512
CHUNKS = SHARED // HID + EXPERTS
PAIRS = CHUNKS // 2
SHARED_PAIRS = SHARED // HID // 2
SCALE = float(D) ** -0.5
EPS = 1e-5
MASKED = -1e30
ROWS = 3 * D
ONE = ROWS

SLOTS = UNITS


def max_pass(s):
    return ((s + 2) % SLOTS, 0 if s < SLOTS - 2 else 1)


def shift_of(s):
    return ((s + 1) % SLOTS, 0 if s < SLOTS - 1 else 1)


def values_of(s):
    return ((s - 1) % SLOTS, 0 if s > 0 else -1)


def placed_in(s):
    return ((s - 3) % SLOTS, 1 if s >= 3 else 0)


def pair_of(s):
    return {5: (0, -1), 6: (1, -1), 0: (2, -2), 1: (3, -2), 2: (4, -2), 3: (5, -2)}.get(s)


EARLY = [("xT", 1), ("tokens3", -1), ("yT", -1), ("vc", 0), None, ("v", 1), ("qkc", 1), None]
LATE = [("tokens2", -1), ("qk", 1), ("out", -1), ("x2T", -1), ("cT", 1), ("route", -1), ("tokens0", 0), ("tokens1", 0)]
C_USES = [use for s in range(SLOTS)
          for use in (EARLY[s], (f"place{placed_in(s)[0]}", placed_in(s)[1]), LATE[s]) if use]

FIRST_USES = [name for name, off in C_USES if off == 1]

Y_USES = [use for s in range(SLOTS)
          for use in ((f"shift{shift_of(s)[0]}", shift_of(s)[1]), (f"value{values_of(s)[0]}", values_of(s)[1]))]


LAST_PAIRS = ([(p, -2) for p in sorted(pair_of(s)[0] for s in range(SLOTS) if pair_of(s) and pair_of(s)[1] == -2)]
              + [(p, -1) for p in range(PAIRS)])
DRAIN = ([("values", 0), ("hidden", 0), ("bank_c", "tokens2"), ("hidden", 1), ("bank_c", "tokens3"), ("w3", 0),
          ("hidden", 2), ("bank_c", "yT"), ("w3", 1), ("hidden", 3), ("bank_c", "out"), ("w3", 2),
          ("warm", 16), ("bank_c", "x2T"), ("w3", 3), ("hidden", 4), ("bank_c", "route"), ("hidden", 5), ("w3", 4)]
         + [(step, i) for k in range(6, 10) for step, i in (("hidden", k), ("w3", k - 1))] + [("w3", 9)])
SETS = 3


WARM_EXP, WARM_MAX, FIRST_WARM = {3: 1, 4: 2, 5: 1}, {4: 1}, 1


class Turn:

    def __init__(self, eng, t, loop):
        self.eng, self.t, self.loop, self.known = eng, t, loop, {}

    def has(self, off):
        return self.loop or 0 <= self.t + off < B

    def at(self, t):
        return not self.loop and self.t == t

    def n(self, off, part=1, of=1):
        if not self.loop:
            return of * (self.t + off) + part
        key = (of, of * off + part)
        if key not in self.known:
            self.known[key] = self.eng.snap(self.t * of + (of * off + part))
        return self.known[key]

    def users_before(self, uses, name):
        at = [u[0] for u in uses].index(name)
        found, wrapped = [], False
        for back in range(1, 2 * len(uses)):
            turns, i = divmod(at - back, len(uses))
            off = uses[i][1] + turns
            if self.has(off) and not self.at(-1) or self.at(-1) and turns == 0 and uses[i][1] == 1:
                wrapped = wrapped or (not found and turns < 0)
                found.append((uses[i][0], off))
        return found, wrapped


def wait(eng, sem, n):
    if not isinstance(n, int) or n > 0:
        eng.wait_ge(sem, n)


def wait_apart(eng, sem, n, passed):
    wait(eng, sem, n)
    eng.sem_inc(passed, 1)


def turns(eng, one_turn, drain=None):
    for t in (-1, 0, 1):
        one_turn(Turn(eng, t, False))
    with eng.Fori(2, B - 2) as t:
        one_turn(Turn(eng, t, True))
    for t in (B - 2, B - 1):
        one_turn(Turn(eng, t, False))
    if drain:
        drain(Turn(eng, B, False))
    else:
        for t in (B, B + 1):
            one_turn(Turn(eng, t, False))


def attention_moe_program(nc, x, ctx_in, Wk, bk, Wq, bq, Wv, bv, Wck, bck, Wcq, bcq, Wcv, bcv, Wp, bp,
                          w12, w3, shared_w1, shared_w2, shared_w3, router_w, expert_bias, out):
    with ExitStack() as stack:
        def sb(name, shape, dt=F32):
            return stack.enter_context(nc.sbuf_tensor(name, shape, dt))

        def sem(name):
            return stack.enter_context(nc.semaphore(name))

        ident = sb("ident", [P, P])
        ident_bf = sb("ident_bf", [P, P], BF16)
        causal = sb("causal", [P, P], BF16)
        sel_build = sb("sel_build", [P, 4, NG, P])
        sel = sb("sel", [P, 4, NG, P], F32R)
        one_build = sb("one_build", [P, GH])
        one_row = sb("one_row", [P, 1])
        minus_one_row = sb("minus_one_row", [P, 1])
        half_power = sb("half_power", [P, NT])
        earlier = sb("earlier", [P, EXPERTS, EXPERTS])
        wx = sb("wx", [P, 4, C])
        wx_hi = sb("wx_hi", [P, 4, C], F32R)
        wx_lo = sb("wx_lo", [P, 4, C], F32R)
        wc = sb("wc", [CC, 2, C])
        wc_hi = sb("wc_hi", [CC, 2, C], F32R)
        wc_lo = sb("wc_lo", [CC, 2, C], F32R)
        wp = sb("wp", [P, C])
        bias_col = sb("bias_col", [P, 4])
        bias_row = sb("bias_row", [P, 3, C])
        ebias = sb("ebias", [P, EXPERTS])
        router_raw = sb("router_raw", [EXPERTS, C])
        router_hi = sb("router_hi", [P, EXPERTS], F32R)
        router_lo = sb("router_lo", [P, EXPERTS], F32R)
        w12_raw = sb("w12_raw", [P, PAIRS, 2, 2, C])
        w12_hi = sb("w12_hi", [P, PAIRS, 2, 2, HID], F32R)
        w12_lo = sb("w12_lo", [P, PAIRS, 2, 2, HID], F32R)
        w3_raw = sb("w3_raw", [P, CHUNKS, HID])
        w3T = sb("w3T", [P, CHUNKS, C])

        xin = sb("xin", [P, NT, C])
        stats1 = sb("stats1", [P, NT, 6])
        mv1 = sb("mv1", [P, NT, 2])
        var1 = sb("var1", [P, NT])
        rstd1 = sb("rstd1", [P, NT])
        xn = sb("xn", [P, NT, C])
        xT = sb("xT", [P, 2, T], F32R)
        cin = sb("cin", [P, NT, C])
        cT = sb("cT", [CC, 2, T], F32R)
        nat = sb("nat", [P, 2, 4, T], F32R)
        qk = sb("qk", [P, UNITS, 2, T], F32R)
        vs = sb("vs", [P, 2, NT, H, QUAD])
        shifts = sb("shifts", [P, NT, P])
        probs = [sb(f"probs{i}", [P, GH, 2 * T]) for i in range(2)]
        yT = sb("yT", [P, UNITS, T])
        recip = sb("recip", [P, H])
        y_tok = sb("y_tok", [P, 2, NT, C])
        y_sum = sb("y_sum", [P, NT, C])
        y_sumT = sb("y_sumT", [P, T])
        xres = sb("xres", [P, NT, C])
        xresb = sb("xresb", [P, NT, C])
        x1 = sb("x1", [P, NT, C])
        stats2 = sb("stats2", [P, NT, 6])
        mv2 = sb("mv2", [P, NT, 2])
        var2 = sb("var2", [P, NT])
        rstd2 = sb("rstd2", [P, NT])
        x2n = sb("x2n", [P, NT, C])
        x2T = sb("x2T", [P, 2, T], F32R)
        route_t = sb("route_t", [P, NT, EXPERTS])
        score = sb("score", [P, NT, EXPERTS])
        biased = sb("biased", [P, NT, EXPERTS])
        above = sb("above", [P, NT, EXPERTS, EXPERTS])
        tied = sb("tied", [P, NT, EXPERTS, EXPERTS])
        rank = sb("rank", [P, NT, EXPERTS])
        gates = sb("gates", [P, NT, EXPERTS])
        th = [sb(f"th{i}", [P, 2 * T]) for i in range(SETS)]
        act1 = [sb(f"act1{i}", [P, 2 * T]) for i in range(SETS)]
        hid = [sb(f"hid{i}", [P, 2, T]) for i in range(SETS)]
        acc = sb("acc", [P, NT, C])

        S = stack.enter_context(nc.psum_tensor("S", [P, GH, 512], F32))
        A = stack.enter_context(nc.psum_tensor("A", [P, 512], F32))
        Bk = stack.enter_context(nc.psum_tensor("Bk", [P, 512], F32))
        Cb = stack.enter_context(nc.psum_tensor("Cb", [P, 512], F32))
        Y = stack.enter_context(nc.psum_tensor("Y", [P, T], F32))

        pair_banks = [(A[:, :], Bk[:, :])] + [(S[:, 2 * k, :], S[:, 2 * k + 1, :]) for k in range(SETS - 1)]

        w_attn_in = sem("w_attn_in")
        w_bias_in = sem("w_bias_in")
        w_ffn_in = sem("w_ffn_in")
        consts = sem("consts")
        w_split = sem("w_split")
        consts_dve = sem("consts_dve")
        sel_ready = sem("sel_ready")
        raw_T = sem("raw_T")
        raw_hi = sem("raw_hi")
        raw_lo = sem("raw_lo")

        dve_passed = sem("dve_passed")
        pool_passed = sem("pool_passed")
        x_in = sem("x_in")
        c_in = sem("c_in")
        xres_in = sem("xres_in")
        out_sent = sem("out_sent")

        scores = [sem(f"scores{u}") for u in range(UNITS)]
        shift_T = [sem(f"shift_T{u}") for u in range(UNITS)]
        stacked = [sem(f"stacked{u}") for u in range(UNITS)]
        valued = [sem(f"valued{u}") for u in range(UNITS)]
        ffn = [sem(f"ffn{p}") for p in range(PAIRS)]
        exped = [sem(f"exped{u}") for u in range(UNITS)]
        qk_ready = [sem(f"qk_ready{u}") for u in range(UNITS)]
        yT_ready = [sem(f"yT_ready{u}") for u in range(UNITS)]
        ffn_th = [sem(f"ffn_th{p}") for p in range(PAIRS)]
        reduced = [sem(f"reduced{u}") for u in range(UNITS)]
        shifted = [sem(f"shifted{u}") for u in range(UNITS)]
        ffn_h1 = [sem(f"ffn_h1{p}") for p in range(PAIRS)]
        hid_ready = [sem(f"hid_ready{p}") for p in range(PAIRS)]
        summed = [sem(f"summed{p}") for p in range(PAIRS)]
        SUM_STEPS = [1] * SHARED_PAIRS + [2 * NT] * (PAIRS - SHARED_PAIRS)
        masked = [sem(f"masked{u}") for u in range(NG)]

        ln1 = sem("ln1")
        rstd1_ready = sem("rstd1_ready")
        xT_ps, xT_hi, xT_lo = sem("xT_ps"), sem("xT_hi"), sem("xT_lo")
        cT_ps, cT_hi, cT_lo = sem("cT_ps"), sem("cT_hi"), sem("cT_lo")
        proj_ps = [sem("proj_x_ps"), sem("proj_c_ps")]
        proj_hi = [sem("proj_x_hi"), sem("proj_c_hi")]
        proj_lo = [sem("proj_x_lo"), sem("proj_c_lo")]
        v_ps = [sem("v_ps"), sem("vc_ps")]
        v_ready = [sem("v_ready"), sem("vc_ready")]
        tokens = sem("tokens")
        recip_ready = sem("recip_ready")
        normed = sem("normed")
        y_summed = sem("y_summed")
        yT_ps, yT_sb = sem("yT_ps"), sem("yT_sb")
        xresb_ready = sem("xresb_ready")
        out_ps = sem("out_ps")
        ln2 = sem("ln2")
        rstd2_ready = sem("rstd2_ready")
        x2T_ps, x2T_hi, x2T_lo = sem("x2T_ps"), sem("x2T_hi"), sem("x2T_lo")
        route_ps, route_th = sem("route_ps"), sem("route_th")
        routed = sem("routed")

        c_free = {f"place{u}": (qk_ready[u], 1, 1) for u in range(UNITS)}
        c_free |= {f"tokens{i}": (normed, i + 1, 4) for i in range(4)}
        c_free |= {"xT": (xT_lo, 1, 1), "vc": (v_ready[1], 1, 1), "v": (v_ready[0], 1, 1),
                   "yT": (yT_sb, 1, 1), "qk": (proj_lo[0], 2, 2), "qkc": (proj_lo[1], 2, 2),
                   "out": (ln2, 1, 7), "cT": (cT_lo, 1, 1), "x2T": (x2T_lo, 1, 1),
                   "route": (route_th, 1, 1)}
        y_free = {f"shift{u}": (shifted[u], 1, 1) for u in range(UNITS)}
        y_free |= {f"value{u}": (yT_ready[u], 1, 1) for u in range(UNITS)}

        def wait_bank(eng, turn, uses, free, name):
            found, wrapped = turn.users_before(uses, name)
            if uses is C_USES and turn.at(-1):
                found = found[1:2]
            elif uses is C_USES and turn.at(0) and wrapped:
                found = found[0:2]
            else:
                found = found[0:1]
            for before, off in found:
                s, part, of = free[before]
                wait(eng, s, turn.n(off, part, of))

        def bank_of(turn, name):
            return A if turn.at(-1) and FIRST_USES.index(name) % 2 else Cb

        def kept(u):
            return 3 * P if u < NG else 4 * P

        RAW_BANKS = PAIRS + CHUNKS // 4
        N_CONSTS = 7

        def raw_banks(s):
            return [s] if s < SLOTS - 1 else list(range(s, RAW_BANKS))

        block = stack.enter_context(nc.Block())

        @block.sync
        def _(sp):
            def load_x(b):
                sp.dma_start(xin[:, :, :], x[b].rearrange("(t p) c -> p t c", p=P)).then_inc(x_in, 16)

            def load_c(b):
                sp.dma_start(cin[:, :, 0:CC], ctx_in[b].rearrange("(t p) c -> p t c", p=P)).then_inc(c_in, 16)

            load_x(0)
            for i, w in enumerate((Wq, Wk, Wcq, Wv)):
                sp.dma_start(wx[:, i, :], w).then_inc(w_attn_in, 16)
            load_c(0)
            for i, w in enumerate((Wck, Wcv)):
                sp.dma_start(wc[:, i, :], w).then_inc(w_attn_in, 16)
            sp.dma_start(wp[:, :], Wp).then_inc(w_ffn_in, 16)
            sp.dma_start(router_raw[:, :], router_w).then_inc(w_ffn_in, 16)
            for j, w in enumerate((shared_w1, shared_w2)):
                for c in range(2):
                    sp.dma_start(w12_raw[:, 0:SHARED_PAIRS, j, c],
                                 w.rearrange("(a c p) i -> c p a i", p=P, c=2)[c]).then_inc(w_ffn_in, 16)
            for j in range(2):
                for c in range(2):
                    sp.dma_start(w12_raw[:, SHARED_PAIRS:PAIRS, j, c],
                                 w12.rearrange("(a c) (j p) i -> j c p a i", p=P, c=2)[j, c]).then_inc(w_ffn_in, 16)
            sp.dma_start(w3_raw[:, 0:SHARED // HID, :],
                         shared_w3.rearrange("d (c h) -> d c h", h=HID)).then_inc(w_ffn_in, 16)
            sp.dma_start(w3_raw[:, SHARED // HID:CHUNKS, :], w3.rearrange("e d h -> d e h")).then_inc(w_ffn_in, 16)

            def one_turn(turn):
                t = turn.t
                if turn.loop or 0 <= t + 2 < B:
                    wait(sp, ln1, turn.n(1, 6, 6))
                    load_x(t + 2)
                if turn.has(-2):
                    wait(sp, summed[PAIRS - 1], turn.n(-2, SUM_STEPS[-1], SUM_STEPS[-1]))
                    sp.dma_start(out[t - 2].rearrange("(t p) c -> p t c", p=P), acc[:, :, :]).then_inc(out_sent, 16)
                if turn.loop or 0 <= t + 2 < B:
                    wait(sp, cT_ps, turn.n(1))
                    load_c(t + 2)
                if turn.has(0):
                    wait(sp, xresb_ready, turn.n(-1))
                    sp.dma_start(xres[:, :, :], x[t].rearrange("(t p) c -> p t c", p=P)).then_inc(xres_in, 16)

            turns(sp, one_turn)
            sp.wait_ge(out_sent, 16 * B)

        @block.tensor
        def _(pe):
            def parts(dst, pairs_):
                for i, (a, m) in enumerate(pairs_):
                    mm = nc.tensor.matmul(dst, a, m, start=(i == 0), stop=(i == len(pairs_) - 1))
                return mm

            def three(w_hi, w_lo, m_hi, m_lo):
                return [(w_hi, m_hi), (w_hi, m_lo), (w_lo, m_hi)]

            def raw_bank(i):
                if i == 0:
                    pe.wait_ge(w_ffn_in, 16 * 12)
                    nc.tensor.transpose(Bk[:, 0:EXPERTS], router_raw[:, :], ident[0:EXPERTS, 0:EXPERTS])
                wait(pe, raw_hi, i)
                wait(pe, raw_lo, min(i, PAIRS))
                for k in range(4):
                    block_ = (w12_raw[:, i, k // 2, k % 2, :] if i < PAIRS else w3_raw[:, 4 * (i - PAIRS) + k, :])
                    mm = nc.tensor.transpose(A[:, k * P:(k + 1) * P], block_, ident[:, :])
                mm.then_inc(raw_T, 1)

            def exp_scores(u, half):
                for j in (2 * half, 2 * half + 1):
                    r = slice(QUAD * j, QUAD * j + ONE + 1)
                    nc.tensor.matmul(S[:, j, 0:T], qk[r, u, 1, 0:P], qk[r, u, 0, :], start=True, stop=True)
                    q0 = P if u < NG else 0
                    mm = nc.tensor.matmul(S[:, j, T:2 * T - q0], qk[r, u, 1, P:T], qk[r, u, 0, q0:T],
                                          start=False, stop=True, skip_group_check=True)
                return mm

            def max_scores(u, half):
                js = (2 * half, 2 * half + 1)
                for j in js:
                    r = slice(QUAD * j, QUAD * j + ROWS)
                    if u < NG:
                        nc.tensor.matmul(S[:, j, T:T + P], qk[r, u, 0, 0:P], qk[r, u, 1, 0:P], start=True, stop=True)
                        mm = nc.tensor.matmul(S[:, j, 0:T], qk[r, u, 0, P:T], qk[r, u, 1, :],
                                              start=False, stop=True, skip_group_check=True)
                    else:
                        for q in range(NT):
                            mm = nc.tensor.matmul(S[:, j, q * T:(q + 1) * T], qk[r, u, 0, q * P:(q + 1) * P],
                                                  qk[r, u, 1, :], start=(q == 0), stop=True,
                                                  skip_group_check=(q > 0))
                if u < NG:
                    for j in js:
                        mm = nc.tensor.matmul(S[:, j, P:3 * P], ident_bf[:, :],
                                              causal[:, :].unsqueeze(1).broadcast_to([P, 2, P]),
                                              start=False, stop=True, skip_group_check=True)
                return mm

            pe.wait_ge(consts, 1)

            def fill(bank, n):
                for _ in range(n):
                    nc.tensor.matmul(bank[:, 0:T], ident_bf[:, :], causal[:, :].unsqueeze(1).broadcast_to([P, 2, P]),
                                     start=True, stop=True)

            def keep_warm(turn, s, counts):
                if turn.at(0) and s >= 2 or turn.at(1) and s <= 4:
                    bank, n = Bk, FIRST_WARM
                elif turn.loop or turn.t >= 2 or turn.at(1) and s > 5:
                    bank, n = A, counts.get(s, 0)
                else:
                    return
                fill(bank, n)

            def exp_pass(turn, s):
                if turn.has(0):
                    for half in range(2):
                        if half == 0:
                            wait(pe, shifted[s], turn.n(0))
                        keep_warm(turn, s, WARM_EXP)
                        un, on = shift_of(s)
                        if turn.has(on):
                            wait(pe, reduced[un], turn.n(on, half + 1, 2))
                        else:
                            wait(pe, exped[s - 1], turn.n(0, half + 1, 2))
                        exp_scores(s, half).then_inc(scores[s], 1)

            def hidden(turn, pair, w, i=0):
                p, o = pair
                if w == 0 and p == 0:
                    wait(pe, x2T_hi, turn.n(o))
                    wait(pe, x2T_lo, turn.n(o))
                if w == 0 and p == 0 and turn.at(1):
                    pe.wait_ge(raw_hi, RAW_BANKS)
                    pe.wait_ge(raw_lo, PAIRS)
                if w == 1 and i == 0:
                    if p > 0:
                        wait(pe, summed[p - 1], turn.n(o, SUM_STEPS[p - 1], SUM_STEPS[p - 1]))
                    elif turn.loop or turn.t + o > 0:
                        wait(pe, summed[PAIRS - 1], turn.n(o - 1, SUM_STEPS[-1], SUM_STEPS[-1]))
                bank = pair_banks[i % SETS][w]
                for c in range(2):
                    mm = parts(bank[:, c * T:(c + 1) * T],
                               three(w12_hi[:, p, w, c, :], w12_lo[:, p, w, c, :], x2T[:, 0, :], x2T[:, 1, :]))
                mm.then_inc(ffn[p], 1)

            def shift_rows(turn, s):
                u, o = shift_of(s)
                if turn.has(o):
                    wait(pe, reduced[u], turn.n(o, 2, 2))
                    wait_bank(pe, turn, Y_USES, y_free, f"shift{u}")
                    for qt in range(NT):
                        mm = nc.tensor.transpose(Y[:, qt * P:(qt + 1) * P], shifts[:, qt, :], ident[:, :])
                    mm.then_inc(shift_T[u], 1)

            def maxima(turn, s):
                u, o = max_pass(s)
                if turn.has(o):
                    wait(pe, qk_ready[u], turn.n(o))
                    if turn.at(-1) and u == 0:
                        pe.wait_ge(consts_dve, 3)
                    for half in range(2):
                        keep_warm(turn, s, WARM_MAX)
                        if turn.has(0):
                            wait(pe, exped[s], turn.n(0, half + 1, 2))
                        elif u > 0:
                            wait(pe, reduced[u - 1], turn.n(o, half + 1, 2))
                        max_scores(u, half).then_inc(scores[u], 1)

            def stack_unit(turn, s):
                u, o = placed_in(s)
                if turn.has(o):
                    kind, g = divmod(u, NG)
                    if turn.at(-1):
                        pe.wait_ge(sel_ready, 1)
                    if g == 0:
                        wait(pe, proj_hi[kind], turn.n(o, 2, 2))
                        wait(pe, proj_lo[kind], turn.n(o, 2, 2))
                    wait_bank(pe, turn, C_USES, c_free, f"place{u}")
                    bank = bank_of(turn, f"place{u}")
                    for i in range(2):
                        mm = parts(bank[:, i * T:(i + 1) * T],
                                   [(sel[:, 2 * i + k, g, :], nat[:, kind, 2 * i + k, :]) for k in range(2)])
                    mm.then_inc(stacked[u], 1)

            def values(turn, s):
                u, o = values_of(s)
                if turn.has(o):
                    wait_bank(pe, turn, Y_USES, y_free, f"value{u}")
                    wait(pe, exped[u], turn.n(o, 2, 2))
                    if u < NG:
                        wait(pe, masked[u], turn.n(o))
                    kind, g = divmod(u, NG)
                    if g == 0:
                        wait(pe, v_ready[kind], turn.n(o))
                    for kt in range(NT):
                        for j in range(GH):
                            q0 = P * kt if kind == 0 else 0
                            mm = nc.tensor.matmul(Y[QUAD * j:QUAD * (j + 1), q0:T], vs[:, kind, kt, GH * g + j, :],
                                                  probs[u % 2][:, j, kt * T:(kt + 1) * T - q0],
                                                  start=(kt == 0), stop=(kt == NT - 1))
                    mm.then_inc(valued[u], 1)

            def w3_product(turn, pair, i=0):
                p, o = pair
                wait(pe, hid_ready[p], turn.n(o))
                bank = pair_banks[i % SETS][1]
                if p < SHARED_PAIRS:
                    for tt in range(NT):
                        mm = parts(bank[:, tt * P:(tt + 1) * P],
                                   [(hid[i % SETS][:, c, tt * P:(tt + 1) * P], w3T[:, 2 * p + c, :]) for c in range(2)])
                else:
                    for c in range(2):
                        for tt in range(NT):
                            k = c * NT + tt
                            mm = parts(bank[:, k * P:(k + 1) * P],
                                       [(hid[i % SETS][:, c, tt * P:(tt + 1) * P], w3T[:, 2 * p + c, :])])
                mm.then_inc(ffn[p], 1)

            def bank_c(turn, use):
                if use is None or not turn.has(use[1]):
                    return
                name, o = use
                bank = bank_of(turn, name)
                if name == "xT":
                    wait(pe, ln1, turn.n(o, 6, 6))
                    wait_bank(pe, turn, C_USES, c_free, name)
                    for tt in range(NT):
                        mm = nc.tensor.transpose(bank[:, tt * P:(tt + 1) * P], xn[:, tt, :], ident[:, :])
                    mm.then_inc(xT_ps, 1)
                elif name == "cT":
                    wait(pe, c_in, turn.n(o, 1, 1) * 16 if not turn.loop else turn.n(o, 16, 16))
                    wait_bank(pe, turn, C_USES, c_free, name)
                    for tt in range(NT):
                        mm = nc.tensor.transpose(bank[:, tt * P:(tt + 1) * P], cin[:, tt, :], ident[:, :])
                    mm.then_inc(cT_ps, 1)
                elif name == "x2T":
                    wait(pe, ln2, turn.n(o, 7, 7))
                    wait_bank(pe, turn, C_USES, c_free, name)
                    for tt in range(NT):
                        mm = nc.tensor.transpose(bank[:, tt * P:(tt + 1) * P], x2n[:, tt, :], ident[:, :])
                    mm.then_inc(x2T_ps, 1)
                elif name == "yT":
                    wait(pe, y_summed, turn.n(o))
                    wait_bank(pe, turn, C_USES, c_free, name)
                    for tt in range(NT):
                        mm = nc.tensor.transpose(bank[:, tt * P:(tt + 1) * P], y_sum[:, tt, :], ident[:, :])
                    mm.then_inc(yT_ps, 1)
                elif name in ("qk", "qkc"):
                    kind = 0 if name == "qk" else 1
                    wait(pe, w_split, 3)
                    if kind == 0:
                        wait(pe, xT_hi, turn.n(o))
                        wait(pe, xT_lo, turn.n(o))
                    else:
                        wait(pe, cT_hi, turn.n(o))
                        wait(pe, cT_lo, turn.n(o))
                    wait_bank(pe, turn, C_USES, c_free, name)
                    q = 2 * kind
                    mm = parts(bank[:, 0:T], three(wx_hi[:, q, :], wx_lo[:, q, :], xT[:, 0, :], xT[:, 1, :]))
                    if kind == 0:
                        mm = parts(bank[:, T:2 * T], three(wx_hi[:, 1, :], wx_lo[:, 1, :], xT[:, 0, :], xT[:, 1, :]))
                    else:
                        mm = parts(bank[:, T:2 * T], three(wc_hi[:, 0, :], wc_lo[:, 0, :], cT[:, 0, :], cT[:, 1, :]))
                    mm.then_inc(proj_ps[kind], 1)
                elif name in ("v", "vc"):
                    kind = 0 if name == "v" else 1
                    wait_bank(pe, turn, C_USES, c_free, name)
                    src, wh, wl = ((xT, wx_hi[:, 3, :], wx_lo[:, 3, :]) if kind == 0 else
                                   (cT, wc_hi[:, 1, :], wc_lo[:, 1, :]))
                    for kt in range(NT):
                        hi, lo = (src[:, i, kt * P:(kt + 1) * P] for i in range(2))
                        mm = parts(bank[:, kt * P:(kt + 1) * P], [(hi, wh), (lo, wh), (hi, wl)])
                    mm.then_inc(v_ps[kind], 1)
                elif name.startswith("tokens"):
                    kind, tt = divmod(int(name[-1]), NT)
                    wait(pe, yT_ready[NG * kind + NG - 1], turn.n(o))
                    wait_bank(pe, turn, C_USES, c_free, name)
                    for g in range(NG):
                        mm = nc.tensor.transpose(bank[:, g * P:(g + 1) * P],
                                                 yT[:, NG * kind + g, tt * P:(tt + 1) * P], ident[:, :])
                    mm.then_inc(tokens, 1)
                elif name == "out":
                    wait(pe, yT_sb, turn.n(o))
                    wait_bank(pe, turn, C_USES, c_free, name)
                    for tt in range(NT):
                        mm = parts(bank[:, tt * P:(tt + 1) * P], [(y_sumT[:, tt * P:(tt + 1) * P], wp[:, :])])
                    mm.then_inc(out_ps, 1)
                elif name == "route":
                    wait(pe, x2T_hi, turn.n(o))
                    wait(pe, x2T_lo, turn.n(o))
                    wait_bank(pe, turn, C_USES, c_free, name)
                    for tt in range(NT):
                        hi, lo = (x2T[:, i, tt * P:(tt + 1) * P] for i in range(2))
                        mm = parts(bank[:, tt * EXPERTS:(tt + 1) * EXPERTS],
                                   [(hi, router_hi[:, :]), (lo, router_hi[:, :]), (hi, router_lo[:, :])])
                    mm.then_inc(route_ps, 1)

            def one_turn(turn):
                for s in range(SLOTS):
                    exp_pass(turn, s)
                    if pair_of(s):
                        if turn.has(pair_of(s)[1]):
                            hidden(turn, pair_of(s), 0)
                        bank_c(turn, EARLY[s])
                        if turn.has(pair_of(s)[1]):
                            hidden(turn, pair_of(s), 1)
                        shift_rows(turn, s)
                        maxima(turn, s)
                        stack_unit(turn, s)
                        values(turn, s)
                        if turn.has(pair_of(s)[1]):
                            w3_product(turn, pair_of(s))
                    else:
                        shift_rows(turn, s)
                        stack_unit(turn, s)
                        maxima(turn, s)
                        values(turn, s)
                    if turn.at(0):
                        for i in raw_banks(s):
                            raw_bank(i)
                    bank_c(turn, LATE[s])

            def drain(turn):
                for step, i in DRAIN:
                    if step == "hidden":
                        if 0 < i < SETS:
                            wait(pe, exped[UNITS - 1], turn.n(-1, i, 2))
                        elif i >= SETS:
                            p, o = LAST_PAIRS[i - SETS]
                            wait(pe, summed[p], turn.n(o, SUM_STEPS[p], SUM_STEPS[p]))
                        hidden(turn, LAST_PAIRS[i], 0, i)
                        hidden(turn, LAST_PAIRS[i], 1, i)
                    elif step == "w3":
                        w3_product(turn, LAST_PAIRS[i], i)
                    elif step == "values":
                        values(turn, 0)
                    elif step == "warm":
                        fill(Y, i)
                    else:
                        bank_c(turn, (i, -1))

            turns(pe, one_turn, drain)

        @block.scalar
        def _(act):
            for i, b_ in enumerate((bq, bk, bcq, bck)):
                act.dma_start(bias_col[:, i:i + 1], b_.rearrange("(c a) -> c a", a=1)).then_inc(w_bias_in, 16)
            for i, b_ in enumerate((bv, bcv, bp)):
                act.dma_start(bias_row[:, i, :], b_.rearrange("(a c) -> a c", a=1).broadcast_to([P, C])).then_inc(w_bias_in, 16)
            act.dma_start(ebias[:, :], expert_bias.rearrange("(a c) -> a c", a=1).broadcast_to([P, EXPERTS])).then_inc(w_bias_in, 16)
            act.wait_ge(consts, 5)
            nc.scalar.copy(sel[:, :, :, :].rearrange("p a g m -> p (a g m)"),
                           sel_build[:, :, :, :].rearrange("p a g m -> p (a g m)")).then_inc(sel_ready, 1)
            act.wait_ge(w_bias_in, 16 * 8)

            def from_bank_c(turn, use):
                if use is None or not turn.has(use[1]):
                    return
                name, o = use
                bank = bank_of(turn, name)
                if name == "cT":
                    wait(act, cT_ps, turn.n(o))
                    nc.scalar.copy(cT[:, 0, :], bank[0:CC, 0:T]).then_inc(cT_hi, 1)
                elif name == "x2T":
                    wait(act, x2T_ps, turn.n(o))
                    nc.scalar.copy(x2T[:, 0, :], bank[:, 0:T]).then_inc(x2T_hi, 1)
                elif name == "qk":
                    wait(act, proj_ps[0], turn.n(o))
                    for i in range(2):
                        nc.scalar.activation(nat[:, 0, 2 * i, :], bank[:, i * T:(i + 1) * T], ACT.Identity,
                                             bias=bias_col[:, i:i + 1]).then_inc(proj_hi[0], 1)
                elif name == "route":
                    wait(act, route_ps, turn.n(o))
                    nc.scalar.activation(route_t[:, :, :].rearrange("p t e -> p (t e)"), bank[:, 0:NT * EXPERTS],
                                         ACT.Tanh, scale=0.5).then_inc(route_th, 1)

            def tanh_h1(turn, pair, i=0):
                p, o = pair
                wait(act, ffn[p], turn.n(o, 1, 3))
                nc.scalar.activation(th[i % SETS][:, :], pair_banks[i % SETS][0], ACT.Tanh, scale=0.5).then_inc(ffn_th[p], 1)

            def values(turn, s):
                u, o = values_of(s)
                if turn.has(o):
                    wait(act, valued[u], turn.n(o))
                    nc.scalar.copy(yT[:, u, :], Y[:, :]).then_inc(yT_ready[u], 1)

            def one_turn(turn):
                for s in range(SLOTS):
                    if turn.has(0):
                        for half in range(2):
                            hs = slice(2 * half, 2 * half + 2)
                            wait(act, scores[s], turn.n(0, 3 + half, 4))
                            if half == 0:
                                v, o = values_of(s - 1) if s > 0 else (SLOTS - 2, -1)
                                wait(act, valued[v], turn.n(o if s != 1 else -1))
                            nc.scalar.activation(probs[s % 2][:, hs, 0:kept(s)], S[:, hs, 0:kept(s)], ACT.Exp,
                                                 scale=SCALE).then_inc(exped[s], 1)
                    if pair_of(s) and turn.has(pair_of(s)[1]):
                        tanh_h1(turn, pair_of(s))
                    u, o = placed_in(s)
                    if turn.has(o):
                        wait(act, stacked[u], turn.n(o))
                        if turn.at(-1) and u == 0:
                            act.wait_ge(consts_dve, 1)
                        nc.scalar.activation(qk[:, u, :, :], bank_of(turn, f"place{u}")[:, :].rearrange("p (i t) -> p i t", i=2), ACT.Identity,
                                             bias=one_row[:, 0:1]).then_inc(qk_ready[u], 1)
                    values(turn, s)
                    if turn.at(0):
                        for i in raw_banks(s):
                            act.wait_ge(raw_T, i + 1)
                            if i == 0:
                                nc.scalar.copy(router_hi[:, :], Bk[:, 0:EXPERTS]).then_inc(consts_dve, 1)
                            if i < PAIRS:
                                nc.scalar.copy(w12_hi[:, i].rearrange("p a b i -> p (a b i)"), A[:, :]).then_inc(raw_hi, 1)
                            else:
                                k = 4 * (i - PAIRS)
                                nc.scalar.mul(w3T[:, k:k + 4, :].rearrange("p k i -> p (k i)"), A[:, :], 0.5).then_inc(raw_hi, 1)
                    from_bank_c(turn, LATE[s])

            def drain(turn):
                for step, i in DRAIN:
                    if step == "hidden":
                        tanh_h1(turn, LAST_PAIRS[i], i)
                    elif step == "values":
                        values(turn, 0)
                    elif step == "bank_c":
                        from_bank_c(turn, (i, -1))

            turns(act, one_turn, drain)

        @block.vector
        def _(dve):
            def low_part(dst, src, hi):
                return nc.vector.tensor_tensor(dst, src, hi.bitcast(F32), ALU.subtract)

            def normalise(turn, off, done, base, of, src, stats, mv, dst, rstd_ready, rstd, first):
                if first:
                    for tt in range(NT):
                        nc.vector.bn_stats(stats[:, tt, :], src[:, tt, :]).then_inc(done, 1)
                    for tt in range(NT):
                        wait_apart(dve, done, turn.n(off, base + tt + 1, of), dve_passed)
                        nc.vector.bn_aggr(mv[:, tt, :], stats[:, tt, :]).then_inc(done, 1)
                else:
                    wait(dve, rstd_ready, turn.n(off, 2, 2))
                    for tt in range(NT):
                        nc.vector.tensor_scalar(dst[:, tt, :], src[:, tt, :], mv[:, tt, 0:1], rstd[:, tt:tt + 1],
                                                ALU.subtract, ALU.mult).then_inc(done, 1)

            def from_bank_c(turn, use):
                if use is None or not turn.has(use[1]):
                    return
                name, o = use
                bank = bank_of(turn, name)
                if name == "xT":
                    wait(dve, xT_ps, turn.n(o))
                    nc.vector.tensor_copy(xT[:, 0, :], bank[:, 0:T]).then_inc(xT_hi, 1)
                    wait(dve, xT_hi, turn.n(o))
                    low_part(xT[:, 1, :], bank[:, 0:T], xT[:, 0, :]).then_inc(xT_lo, 1)
                elif name == "cT":
                    wait(dve, cT_hi, turn.n(o))
                    low_part(cT[:, 1, :], bank[0:CC, 0:T], cT[:, 0, :]).then_inc(cT_lo, 1)
                elif name == "x2T":
                    wait(dve, x2T_hi, turn.n(o))
                    low_part(x2T[:, 1, :], bank[:, 0:T], x2T[:, 0, :]).then_inc(x2T_lo, 1)
                elif name in ("qk", "qkc"):
                    kind = 0 if name == "qk" else 1
                    if kind == 1:
                        wait(dve, proj_ps[1], turn.n(o))
                        for i in range(2):
                            nc.vector.tensor_scalar(nat[:, 1, 2 * i, :], bank[:, i * T:(i + 1) * T],
                                                    bias_col[:, 2 + i:3 + i], None, ALU.add).then_inc(proj_hi[1], 1)
                    for i in range(2):
                        wait(dve, proj_hi[kind], turn.n(o, 2, 2))
                        nc.vector.scalar_tensor_tensor(
                            out=nat[:, kind, 2 * i + 1, :], in0=bank[:, i * T:(i + 1) * T],
                            scalar=bias_col[:, 2 * kind + i:2 * kind + i + 1], in1=nat[:, kind, 2 * i, :].bitcast(F32),
                            op0=ALU.add, op1=ALU.subtract).then_inc(proj_lo[kind], 1)
                elif name == "yT":
                    wait(dve, yT_ps, turn.n(o))
                    nc.vector.tensor_copy(y_sumT[:, :], bank[:, 0:T]).then_inc(yT_sb, 1)
                elif name in ("v", "vc"):
                    kind = 0 if name == "v" else 1
                    wait(dve, v_ps[kind], turn.n(o))
                    if not turn.loop and turn.t + o == 0:
                        dve.wait_ge(consts, N_CONSTS)
                    for kt in range(NT):
                        r_ = nc.vector.tensor_tensor(
                            vs[:, kind, kt, :, 0:D], bank[:, kt * P:(kt + 1) * P].rearrange("p (h d) -> p h d", d=D),
                            bias_row[:, kind, :].rearrange("p (h d) -> p h d", d=D), ALU.add)
                    r_.then_inc(v_ready[kind], 1)
                elif name.startswith("tokens"):
                    i = int(name[-1])
                    kind, tt = divmod(i, NT)
                    wait(dve, tokens, turn.n(o, i + 1, 4))
                    heads = bank[:, :].rearrange("p (h r) -> p h r", r=QUAD)
                    nc.vector.reciprocal(recip[:, :], heads[:, :, D]).then_inc(recip_ready, 1)
                    wait(dve, recip_ready, turn.n(o, i + 1, 4))
                    nc.vector.tensor_tensor(y_tok[:, kind, tt, :].rearrange("p (h d) -> p h d", d=D),
                                            heads[:, :, 0:D],
                                            recip[:, :].unsqueeze(2).broadcast_to([P, H, D]),
                                            ALU.mult).then_inc(normed, 1)
                elif name == "out":
                    wait(dve, out_ps, turn.n(o))
                    wait(dve, xresb_ready, turn.n(o))
                    nc.vector.tensor_tensor(x1[:, :, :].rearrange("p t c -> p (t c)"), bank[:, 0:T],
                                            xresb[:, :, :].rearrange("p t c -> p (t c)"), ALU.add).then_inc(ln2, 1)
                    wait(dve, ln2, turn.n(o, 1, 7))
                    normalise(turn, o, ln2, 1, 7, x1, stats2, mv2, x2n, rstd2_ready, rstd2, True)
                elif name == "route":
                    wait(dve, route_th, turn.n(o))
                    nc.vector.tensor_scalar(score[:, :, :], route_t[:, :, :], 0.5, 0.5, ALU.mult,
                                            ALU.add).then_inc(routed, 1)
                    wait(dve, routed, turn.n(o, 1, 8))
                    nc.vector.tensor_tensor(biased[:, :, :], score[:, :, :],
                                            ebias[:, :].unsqueeze(1).broadcast_to([P, NT, EXPERTS]),
                                            ALU.add).then_inc(routed, 1)
                    wait(dve, routed, turn.n(o, 2, 8))
                    for tt in range(NT):
                        mine = biased[:, tt, :].unsqueeze(2).broadcast_to([P, EXPERTS, EXPERTS])
                        other = biased[:, tt, :].unsqueeze(1).broadcast_to([P, EXPERTS, EXPERTS])
                        nc.vector.tensor_tensor(above[:, tt], other, mine, ALU.is_gt)
                        r_ = nc.vector.tensor_tensor(tied[:, tt], other, mine, ALU.is_equal)
                    r_.then_inc(routed, 1)
                    wait(dve, routed, turn.n(o, 3, 8))
                    nc.vector.tensor_tensor(tied[:, :, :, :], tied[:, :, :, :],
                                            earlier[:, :, :].unsqueeze(1).broadcast_to([P, NT, EXPERTS, EXPERTS]),
                                            ALU.mult).then_inc(routed, 1)
                    wait(dve, routed, turn.n(o, 4, 8))
                    nc.vector.tensor_tensor(above[:, :, :, :], above[:, :, :, :], tied[:, :, :, :],
                                            ALU.add).then_inc(routed, 1)
                    wait(dve, routed, turn.n(o, 5, 8))
                    nc.vector.reduce_sum(rank[:, :, :], above[:, :, :, :], AX_X).then_inc(routed, 1)
                    wait(dve, routed, turn.n(o, 6, 8))
                    nc.vector.tensor_scalar(rank[:, :, :], rank[:, :, :], 2.0, None, ALU.is_lt).then_inc(routed, 1)
                    wait(dve, routed, turn.n(o, 7, 8))
                    nc.vector.tensor_tensor(gates[:, :, :], rank[:, :, :], score[:, :, :],
                                            ALU.mult).then_inc(routed, 1)

            def activate(turn, pair, i=0):
                p, o = pair
                wait(dve, ffn_th[p], turn.n(o))
                nc.vector.scalar_tensor_tensor(out=act1[i % SETS][:, :], in0=th[i % SETS][:, :], scalar=1.0,
                                               in1=pair_banks[i % SETS][0],
                                               op0=ALU.add, op1=ALU.mult).then_inc(ffn_h1[p], 1)

            def times_h2(turn, pair, i=0):
                p, o = pair
                wait(dve, ffn_h1[p], turn.n(o))
                wait(dve, ffn[p], turn.n(o, 2, 3))
                nc.vector.tensor_tensor(hid[i % SETS][:, :, :].rearrange("p c t -> p (c t)"), act1[i % SETS][:, :],
                                        pair_banks[i % SETS][1], ALU.mult).then_inc(hid_ready[p], 1)

            def add_up(turn, pair, i=0):
                p, o = pair
                bank = pair_banks[i % SETS][1]
                wait(dve, ffn[p], turn.n(o, 3, 3))
                if p < SHARED_PAIRS:
                    if p == 0:
                        wait(dve, out_sent, turn.n(o - 1, 16, 16))
                    else:
                        wait(dve, summed[p - 1], turn.n(o))
                    before = x1 if p == 0 else acc
                    nc.vector.tensor_tensor(acc[:, :, :].rearrange("p t c -> p (t c)"), bank[:, 0:T],
                                            before[:, :, :].rearrange("p t c -> p (t c)"),
                                            ALU.add).then_inc(summed[p], 1)
                else:
                    if p == SHARED_PAIRS:
                        wait(dve, routed, turn.n(o, 8, 8))
                        wait(dve, summed[p - 1], turn.n(o))
                    else:
                        wait(dve, summed[p - 1], turn.n(o, 4, 4))
                    for c in range(2):
                        for tt in range(NT):
                            k = c * NT + tt
                            e = 2 * (p - SHARED_PAIRS) + c
                            if c == 1:
                                wait(dve, summed[p], turn.n(o, tt + 1, 4))
                            nc.vector.scalar_tensor_tensor(out=acc[:, tt, :], in0=bank[:, k * P:(k + 1) * P],
                                                           scalar=gates[:, tt, e:e + 1], in1=acc[:, tt, :],
                                                           op0=ALU.mult, op1=ALU.add).then_inc(summed[p], 1)

            first = Turn(dve, 0, False)
            dve.wait_ge(x_in, 16)
            normalise(first, 0, ln1, 0, 6, xin, stats1, mv1, xn, rstd1_ready, rstd1, True)
            dve.wait_ge(consts, 4)
            nc.vector.reduce_sum(one_row[:, :], one_build[:, :], AX_X).then_inc(consts_dve, 1)
            dve.wait_ge(consts_dve, 1)
            nc.vector.tensor_scalar(minus_one_row[:, :], one_row[:, :], -1.0, None, ALU.mult).then_inc(consts_dve, 1)
            nc.vector.tensor_copy(ident_bf[:, :], ident[:, :]).then_inc(consts_dve, 1)
            normalise(first, 0, ln1, 0, 6, xin, stats1, mv1, xn, rstd1_ready, rstd1, False)
            dve.wait_ge(w_attn_in, 16 * 6)
            nc.vector.tensor_copy(wx_hi[:, :, :].rearrange("p a c -> p (a c)"),
                                  wx[:, :, :].rearrange("p a c -> p (a c)")).then_inc(w_split, 1)
            nc.vector.tensor_copy(wc_hi[:, :, :].rearrange("p a c -> p (a c)"),
                                  wc[:, :, :].rearrange("p a c -> p (a c)")).then_inc(w_split, 1)
            dve.wait_ge(w_split, 2)
            nc.vector.tensor_tensor(wx_lo[:, :, :], wx[:, :, :], wx_hi[:, :, :].bitcast(F32), ALU.subtract)
            nc.vector.tensor_tensor(wc_lo[:, :, :], wc[:, :, :], wc_hi[:, :, :].bitcast(F32), ALU.subtract).then_inc(w_split, 1)
            dve.wait_ge(w_bias_in, 16 * 8)

            def one_turn(turn):
                for s in range(SLOTS):
                    from_bank_c(turn, EARLY[s])
                    pr = pair_of(s)
                    if pr and turn.has(pr[1]):
                        activate(turn, pr)
                    if s == 7 and turn.has(2):
                        wait(dve, x_in, turn.n(2, 16, 16))
                        normalise(turn, 2, ln1, 0, 6, xin, stats1, mv1, xn, rstd1_ready, rstd1, True)
                    u, o = shift_of(s)
                    if turn.has(o):
                        wait(dve, shift_T[u], turn.n(o))
                        nc.vector.scalar_tensor_tensor(out=qk[:, u, 0, :], in0=Y[:, :], scalar=minus_one_row[:, 0:1],
                                                       in1=qk[:, u, 0, :].bitcast(F32), op0=ALU.add,
                                                       op1=ALU.add).then_inc(shifted[u], 1)
                    if pr and turn.has(pr[1]):
                        times_h2(turn, pr)
                    if s == 3 and turn.has(-1):
                        normalise(turn, -1, ln2, 1, 7, x1, stats2, mv2, x2n, rstd2_ready, rstd2, False)
                    u, o = max_pass(s)
                    if turn.has(o):
                        for half in range(2):
                            hs = slice(2 * half, 2 * half + 2)
                            wait(dve, scores[u], turn.n(o, half + 1, 4))
                            dst = shifts[:, :, :].rearrange("p q (j r) -> p q j r", r=QUAD)[:, :, hs, ONE]
                            if u < NG:
                                nc.vector.tensor_reduce(dst[:, 1, :], S[:, hs, 0:T], AX_X, ALU.max, negate=True)
                                nc.vector.tensor_reduce(dst[:, 0, :], S[:, hs, T:T + P], AX_X, ALU.max,
                                                        negate=True).then_inc(reduced[u], 1)
                            else:
                                nc.vector.tensor_reduce(dst.rearrange("p q j -> p j q"),
                                                        S[:, hs, :].rearrange("p j (q k) -> p j q k", q=NT),
                                                        AX_X, ALU.max, negate=True).then_inc(reduced[u], 1)
                    if pr and turn.has(pr[1]):
                        add_up(turn, pr)
                    if turn.at(0):
                        for i in [i for i in raw_banks(s) if i < PAIRS]:
                            dve.wait_ge(raw_hi, i + 1)
                            if i == 0:
                                low_part(router_lo[:, :], Bk[:, 0:EXPERTS], router_hi[:, :])
                            low_part(w12_lo[:, i].rearrange("p a b i -> p (a b i)"), A[:, :],
                                     w12_hi[:, i].rearrange("p a b i -> p (a b i)")).then_inc(raw_lo, 1)
                    if s == 7 and turn.has(2):
                        wait(dve, xT_ps, turn.n(1))
                        normalise(turn, 2, ln1, 0, 6, xin, stats1, mv1, xn, rstd1_ready, rstd1, False)
                    from_bank_c(turn, LATE[s])

            def drain(turn):
                for step, i in DRAIN:
                    if step == "hidden":
                        activate(turn, LAST_PAIRS[i], i)
                        times_h2(turn, LAST_PAIRS[i], i)
                    elif step == "w3":
                        add_up(turn, LAST_PAIRS[i], i)
                    elif step == "bank_c":
                        if i == "x2T":
                            normalise(turn, -1, ln2, 1, 7, x1, stats2, mv2, x2n, rstd2_ready, rstd2, False)
                        from_bank_c(turn, (i, -1))

            turns(dve, one_turn, drain)

        @block.gpsimd
        def _(pool):
            def select(dst, compare, fill, base, pattern, step):
                return nc.gpsimd.affine_select(out=dst, in_=dst, compare_op=compare, fill=fill, base=base,
                                               pattern=pattern, channel_multiplier=step)

            def rstd(turn, off, stats_done, part, of, mv, var, dst, ready):
                wait_apart(pool, stats_done, turn.n(off, part, of), pool_passed)
                nc.gpsimd.tensor_scalar(var[:, :], mv[:, :, 1], EPS, None, ALU.add).then_inc(ready, 1)
                wait(pool, ready, turn.n(off, 1, 2))
                nc.gpsimd.tensor_tensor(dst[:, :], var[:, :], half_power[:, :], ALU.pow).then_inc(ready, 1)

            built = sem("built")
            nc.gpsimd.memset(ident[:, :], 0.0).then_inc(built, 1)
            nc.gpsimd.memset(one_build[:, :], 0.0).then_inc(built, 1)
            nc.gpsimd.memset(causal[:, :], 0.0).then_inc(built, 1)
            nc.gpsimd.memset(cin[:, :, CC:C], 0.0).then_inc(built, 1)
            nc.gpsimd.memset(shifts[:, :, :], 0.0).then_inc(built, 1)
            nc.gpsimd.memset(sel_build[:, :, :, :], 0.0).then_inc(built, 1)
            pool.wait_ge(built, 1)
            select(ident[:, :], ALU.not_equal, 1.0, 0, [[-1, P]], 1).then_inc(consts, 1)
            pool.wait_ge(built, 5)
            select(one_build[:, :], ALU.not_equal, 1.0, -ONE, [[-QUAD, GH]], 1).then_inc(consts, 1)
            select(causal[:, :], ALU.is_ge, MASKED, 0, [[-1, P]], 1).then_inc(consts, 1)
            nc.gpsimd.memset(half_power[:, :], -0.5).then_inc(consts, 1)
            pool.wait_ge(consts, 4)
            rstd(Turn(pool, 0, False), 0, ln1, 4, 6, mv1, var1, rstd1, rstd1_ready)
            pool.wait_ge(built, 6)
            for part, rows in ((0, (0, 1)), (1, (2,)), (2, (0, 2)), (3, (1,))):
                view = sel_build[:, part, :, :].rearrange("p g (j r) -> p g j r", r=QUAD)
                for r in rows:
                    last = select(view[:, :, :, r * D:(r + 1) * D], ALU.not_equal, 1.0, 0,
                                  [[-GH * D, NG], [-D, GH], [-1, D]], 1)
            last.then_inc(consts, 1)
            nc.gpsimd.memset(vs[:, :, :, :, :], 0.0).then_inc(built, 1)
            nc.gpsimd.memset(earlier[:, :, :], 1.0).then_inc(built, 1)
            pool.wait_ge(built, 8)
            nc.gpsimd.memset(vs[:, :, :, :, D:D + 1], 1.0).then_inc(consts, 1)
            select(earlier[:, :, :], ALU.is_gt, 0.0, 0, [[1, EXPERTS], [-1, EXPERTS]], 0).then_inc(consts, 1)
            pool.wait_ge(w_bias_in, 16 * 8)

            def one_turn(turn):
                for s in range(SLOTS):
                    if s == 3 and turn.has(-1):
                        rstd(turn, -1, ln2, 5, 7, mv2, var2, rstd2, rstd2_ready)
                    if s < NG and turn.has(0):
                        wait_apart(pool, exped[s], turn.n(0, 2, 2), pool_passed)
                        diag = probs[s % 2][:, :, :].rearrange("p h (b q) -> p h b q", b=2)[:, :, :, 0:P]
                        select(diag, ALU.is_ge, 0.0, 0, [[0, GH], [0, 2], [1, P]], -1).then_inc(masked[s], 1)
                    if s == 1 and turn.has(-1):
                        wait(pool, normed, turn.n(-1, 4, 4))
                        nc.gpsimd.tensor_tensor(y_sum[:, :, :], y_tok[:, 0], y_tok[:, 1], ALU.add).then_inc(y_summed, 1)
                        wait(pool, xres_in, turn.n(-1, 16, 16))
                        for tt in range(NT):
                            r_ = nc.gpsimd.tensor_tensor(xresb[:, tt, :], xres[:, tt, :], bias_row[:, 2, :], ALU.add)
                        r_.then_inc(xresb_ready, 1)
                    if s == 7 and turn.has(2):
                        rstd(turn, 2, ln1, 4, 6, mv1, var1, rstd1, rstd1_ready)

            turns(pool, one_turn)


_INS = ['x', 'ctx_512', 'L0_xattn_Wk', 'L0_xattn_bk', 'L0_xattn_Wq', 'L0_xattn_bq', 'L0_xattn_Wv', 'L0_xattn_bv',
        'L0_xattn_Wck', 'L0_xattn_bck', 'L0_xattn_Wcq', 'L0_xattn_bcq', 'L0_xattn_Wcv', 'L0_xattn_bcv', 'L0_xattn_Wp',
        'L0_xattn_bp', 'L0_ffn_w12', 'L0_ffn_w3', 'L0_ffn_shared_w1', 'L0_ffn_shared_w2', 'L0_ffn_shared_w3',
        'L0_ffn_router_w', 'L0_ffn_expert_bias']
_OUT = (B, T, C)


def kernel(**inputs):
    import numpy as _np
    import concourse.bacc as _bacc
    from concourse import mybir as _mybir
    from concourse.bass_utils import run_bass_kernel_spmd as _run

    nc = _bacc.Bacc("TRN2", target_bir_lowering=False, num_devices=1)
    arrays, args = {}, []
    for name in _INS:
        a = _np.ascontiguousarray(inputs[name])
        arrays[f"in_{name}_dram"] = a
        args.append(nc.dram_tensor(f"in_{name}_dram", a.shape, _mybir.dt.from_np(a.dtype), kind="ExternalInput").ap())
    args.append(nc.dram_tensor("out_0_dram", _OUT, _mybir.dt.float32, kind="ExternalOutput").ap())
    attention_moe_program(nc, *args)
    r = _run(nc, [arrays], core_ids=[0])
    return r.results[0]["out_0_dram"]
```
